# Optimizing a Trainium2 kernel written in Bass

```python
import numpy as np
import jax
import jax.numpy as jnp

def _softmax(x, axis=-1):
    return jax.nn.softmax(x, axis=axis)

def _gelu(x):
    return jax.nn.gelu(x, approximate=True)

def _silu(x):
    return jax.nn.silu(x)

def _sigmoid(x):
    return jax.nn.sigmoid(x)

def _layernorm(x, axis=-1, eps=1e-05):
    m = jnp.mean(x, axis=axis, keepdims=True)
    v = jnp.var(x, axis=axis, keepdims=True)
    return (x - m) / jnp.sqrt(v + eps)

def _scatter_add(tgt, idx, src, axis=0):
    return tgt.at[idx].add(src)

def _segment_sum(src, seg, n):
    return jax.ops.segment_sum(src, seg, n)
kernel_name = 'mk_adj_resnorm_d2_adj_r2_a6fed8'

def setup_inputs(seed: int=0):
    np.random.seed(seed)
    _w = jnp.asarray

    def _rec_inputs():
        import jax
        import jax.numpy as jnp
        _gk = jax.random.key(seed)
        x = -0.0005207 + 1.001 * jax.random.normal(jax.random.fold_in(_gk, 1), (4096, 128), jnp.float32)
        _a = jax.random.bernoulli(jax.random.fold_in(_gk, 2), 0.000976562, (4096, 4096))
        _a = jnp.logical_or(_a, jnp.swapaxes(_a, -1, -2))
        _a = jnp.logical_or(_a, jnp.eye(4096, dtype=bool))
        adj = _a.astype(jnp.int32)
        return (x, adj)
    x, adj = _rec_inputs()

    def _L0_gnn_setup():
        import jax, jax.numpy as jnp
        import numpy as np
        N = 4096
        D_IN = 128
        D_HID = 128
        D_OUT = 128
        key = jax.random.key(seed)
        k_x, k_a, k_q, k_k, k_v = jax.random.split(key, 5)
        X = jax.random.normal(k_x, (N, D_IN), dtype=jnp.float32)
        A = jax.random.randint(k_a, (N, N), 0, 2, dtype=jnp.int32)
        A = A * (1 - jnp.eye(N, dtype=jnp.int32))
        Wq = jax.random.normal(k_q, (D_IN, D_HID), dtype=jnp.float32) / 10.0
        Wk = jax.random.normal(k_k, (D_IN, D_HID), dtype=jnp.float32) / 10.0
        Wv = jax.random.normal(k_v, (D_IN, D_OUT), dtype=jnp.float32) / 10.0
        return {'X': X, 'A': A, 'Wq': Wq, 'Wk': Wk, 'Wv': Wv}
    _L0_gnn_all = _L0_gnn_setup()
    _L0_gnn_in = {k: v for k, v in _L0_gnn_all.items() if k in ('Wq', 'Wk', 'Wv')}
    del _L0_gnn_all

    def _L1_gnn_setup():
        import jax, jax.numpy as jnp
        import numpy as np
        N = 4096
        D_IN = 128
        D_OUT = 128
        NEG_INF = -9000000000000000.0
        key = jax.random.key(seed)
        k1, k2, k3, k4 = jax.random.split(key, 4)
        node_features = jax.random.normal(k1, (N, D_IN), dtype=jnp.float32)
        adjacency_matrix = jax.random.randint(k2, (N, N), 0, 2, dtype=jnp.int32)
        W = jax.random.normal(k3, (D_OUT, D_IN), dtype=jnp.float32) / np.sqrt(D_IN)
        b_W = jnp.zeros((D_OUT,), dtype=jnp.float32)
        a_vec = jax.random.normal(k4, (2 * D_OUT,), dtype=jnp.float32) / np.sqrt(2 * D_OUT)
        b_a = jnp.zeros((1,), dtype=jnp.float32)
        return {'node_features': node_features, 'adjacency_matrix': adjacency_matrix, 'W': W, 'b_W': b_W, 'a_vec': a_vec, 'b_a': b_a}
    _L1_gnn_all = _L1_gnn_setup()
    _L1_gnn_in = {k: v for k, v in _L1_gnn_all.items() if k in ('W', 'b_W', 'a_vec', 'b_a')}
    del _L1_gnn_all
    return {'x': x, 'adj': adj, 'L0_gnn_Wq': _L0_gnn_in['Wq'], 'L0_gnn_Wk': _L0_gnn_in['Wk'], 'L0_gnn_Wv': _L0_gnn_in['Wv'], 'L1_gnn_W': _L1_gnn_in['W'], 'L1_gnn_b_W': _L1_gnn_in['b_W'], 'L1_gnn_a_vec': _L1_gnn_in['a_vec'], 'L1_gnn_b_a': _L1_gnn_in['b_a']}

def reference(x, adj, L0_gnn_Wq, L0_gnn_Wk, L0_gnn_Wv, L1_gnn_W, L1_gnn_b_W, L1_gnn_a_vec, L1_gnn_b_a):
    import jax
    import jax.numpy as jnp

    def _L0_gnn_ref(X, A, Wq, Wk, Wv):
        import jax, jax.numpy as jnp
        import numpy as np
        N = 4096
        D_IN = 128
        D_HID = 128
        D_OUT = 128
        n = A.shape[0]
        Af = A.astype(X.dtype) + jnp.eye(n, dtype=X.dtype)
        Q = X @ Wq
        K = X @ Wk
        V = X @ Wv
        S = Q @ K.T
        mask = jnp.nan_to_num(-jnp.inf * (1.0 - Af), nan=0.0)
        P = jax.nn.softmax(S + mask, axis=1)
        return P @ V

    def _L1_gnn_ref(node_features, adjacency_matrix, W, b_W, a_vec, b_a):
        import jax, jax.numpy as jnp
        import numpy as np
        N = 4096
        D_IN = 128
        D_OUT = 128
        NEG_INF = -9000000000000000.0
        h = node_features @ W.T + b_W
        a1, a2 = (a_vec[:D_OUT], a_vec[D_OUT:])
        e = (h @ a1)[:, None] + (h @ a2)[None, :] + b_a[0]
        e = jnp.where(e > 0, e, 0.2 * e)
        scores = jnp.where(adjacency_matrix > 0, e, jnp.float32(NEG_INF))
        attention = jax.nn.softmax(scores, axis=1)
        h_prime = attention @ h
        return h_prime
    x = _layernorm(x + _L0_gnn_ref(x, adj, L0_gnn_Wq, L0_gnn_Wk, L0_gnn_Wv), axis=-1)
    x = _layernorm(x + _L1_gnn_ref(x, adj, L1_gnn_W, L1_gnn_b_W, L1_gnn_a_vec, L1_gnn_b_a), axis=-1)
    return x

_drawn_inputs = setup_inputs


def setup_inputs(seed=0):
    import zlib

    import numpy as np

    out = dict(_drawn_inputs(seed))
    spreads = {'L1_gnn_b_W': (0.0, 0.1)}
    factors = {}
    for name, (base, spread) in spreads.items():
        noise = np.random.default_rng([zlib.crc32(name.encode()), seed]).standard_normal(out[name].shape)
        drawn = base * np.exp(spread * noise) if base else spread * noise
        out[name] = jnp.asarray(drawn.astype(out[name].dtype))
    for name, factor in factors.items():
        out[name] = (out[name] * factor).astype(out[name].dtype)
    return out
```

```python
from contextlib import ExitStack

import numpy as np
import concourse.bass as bass
from concourse import mybir

F32 = mybir.dt.float32
F16 = mybir.dt.float16
I32 = mybir.dt.int32
U32 = mybir.dt.uint32
U16 = mybir.dt.uint16
ALU = mybir.AluOpType
ACT = mybir.ActivationFunctionType
AX = mybir.AxisListType.X
AXY = mybir.AxisListType.XY

P = 128
EPS = 1e-5
SLOPE = 0.2
LIMIT = 60.0
FLT_MAX = float(np.finfo(np.float32).max)
NEG = 9e15


def graph_layers(nc, x, adj, Wq, Wk, Wv, W, b, a_vec, b_a, out, force_general=False):
    N, D = x.shape
    assert D == P and N % 512 == 0
    T = N // P
    Q = 4
    GW = Q * P
    G = N // GW
    PAIRS = T // 2
    CHUNKS = 4
    CW = N // CHUNKS
    PPC = PAIRS // CHUNKS
    NA = 4
    NE = 4
    AHEAD = 2
    assert PAIRS % NA == 0 and PAIRS % NE == 0
    FIN = 7
    FT = 8
    M0_READY, U_READY, W2_READY = 4, 11, 16
    EXT_READY, DIAG_READY, BIASES = 6, 8, 13
    CHECKS_READY = 9

    x_t = x.rearrange("(t p) d -> p t d", p=P)
    out_t = out.rearrange("(t p) d -> p t d", p=P)
    a1_col = a_vec[0:D].rearrange("(p c) -> p c", c=1)
    a2_col = a_vec[D:2 * D].rearrange("(p c) -> p c", c=1)
    b_col = b.rearrange("(p c) -> p c", c=1)
    b_row = b.rearrange("(a d) -> a d", a=1)
    diagonal = adj.rearrange("i j -> (i j)")[0:N * N:N + 1].rearrange("(t p) -> p t", p=P)
    ba_11 = b_a.rearrange("(a d) -> a d", a=1)

    with ExitStack() as ctx:
        def sb(name, shape, dt=F32):
            return ctx.enter_context(nc.sbuf_tensor(name, shape, dt))

        def sem(name):
            return ctx.enter_context(nc.semaphore(name))

        bank = [ctx.enter_context(nc.psum_tensor(f"bank{i}", [P, 512], F32)) for i in range(8)]
        ps_at = [bank[i][:, :].bitcast(F16) for i in range(NA)]
        ps_at_int = [bank[i][:, :].bitcast(U16) for i in range(NA)]
        ps_acc, ps_out, ps_den, ps_misc = bank[4], bank[5], bank[6], bank[7]

        ident = sb("ident", [P, P])
        ones = sb("ones", [P, P])
        wv = sb("wv", [P, D])
        w_nat = sb("w_nat", [P, D])
        w_t = sb("w_t", [P, D])
        acol = sb("acol", [P, 2])
        bcol = sb("bcol", [P, 1])
        brow = sb("brow", [1, D])
        ba = sb("ba", [1, 1])
        u = sb("u", [P, 2])
        u1_rep = sb("u1_rep", [P, P])
        bb = sb("bb", [P, 1])
        cs = sb("cs", [P, 1])
        flag = sb("flag", [1, 1], I32)
        a_sb = sb("a_sb", [P, Q, N], I32)
        x_sb = sb("x_sb", [P, T, D])
        xhat = sb("xhat", [P, T, D])
        xhat_t = sb("xhat_t", [P, N])
        feat = sb("feat", [P, T, D])
        s_all = sb("s_all", [P, N])
        R = sb("R", [P, GW])
        e_sb = sb("e_sb", [P, NE, 2 * GW])
        x_tr = sb("x_tr", [P, 2, GW])
        sq = sb("sq", [P, 2, GW])
        last_row = sb("last_row", [P, P])
        less_last = sb("less_last", [P, P])
        e_last = sb("e_last", [1, P])
        ident16 = sb("ident16", [P, P], F16)
        m0 = sb("m0", [P, D])
        m0c = sb("m0c", [P, D])
        w2 = sb("w2", [P, D])
        w2c = sb("w2c", [P, D])
        mean = sb("mean", [P, 4])
        ss = sb("ss", [P, 2, Q])
        rv = sb("rv", [P, 2, Q])
        rstd = sb("rstd", [P, 2, Q])
        st_cols = sb("st_cols", [P, T, 2])
        ext = sb("ext", [P, 4])
        ext_max = sb("ext_max", [4, 1])
        ext_diag = sb("ext_diag", [4, 4])
        ext_all = sb("ext_all", [P, 4])
        bias = sb("bias", [P, 4])
        minus1 = sb("minus1", [P, 1])
        minus_half = sb("minus_half", [P, 1])
        w_exp = sb("w_exp", [P, T])
        v_exp = sb("v_exp", [P, T])
        acc_t = sb("acc_t", [P, GW])
        y = sb("y", [P, Q, D])
        ysq = sb("ysq", [P, Q, D])
        rden = sb("rden", [P, Q])
        fss = sb("fss", [P, Q])
        frv = sb("frv", [P, Q])
        frstd = sb("frstd", [P, Q])
        out_sb = sb("out_sb", [P, Q, D])
        diag = sb("diag", [P, T], I32)
        a_sum = sb("a_sum", [P, G * CHUNKS])
        a_junk = sb("a_junk", [P, Q * CW], mybir.dt.bfloat16)
        checks = sb("checks", [P, 5])
        bad_cols = sb("bad_cols", [P, 1])
        bad_row = sb("bad_row", [1, 1])

        params_loaded = sem("params_loaded")
        diag_loaded = sem("diag_loaded")
        x_loaded = [sem(f"x_loaded{i}") for i in range(G // 2)]
        a_loaded = [sem(f"a_loaded{c}") for c in range(CHUNKS)]
        consts_ready = sem("consts_ready")
        vec_const = sem("vec_const")
        pe_const = sem("pe_const")
        xt_ready = sem("xt_ready")
        xt_copied = sem("xt_copied")
        y0_ready = sem("y0_ready")
        sq_ready = sem("sq_ready")
        norm0 = sem("norm0")
        rstd_ready = sem("rstd_ready")
        xhat_ready = sem("xhat_ready")
        xht_ready = sem("xht_ready")
        xht_copied = sem("xht_copied")
        s_ready = sem("s_ready")
        s_copied = sem("s_copied")
        stat = sem("stat")
        stat_pe = sem("stat_pe")
        exps_ready = sem("exps_ready")
        feat_ready = sem("feat_ready")
        at_ready = sem("at_ready")
        e_ready = sem("e_ready")
        p_ready = sem("p_ready")
        mm_done = sem("mm_done")
        a_checked = sem("a_checked")
        acc_copied = sem("acc_copied")
        fin_mm = sem("fin_mm")
        fin_step = sem("fin_step")
        stored = sem("stored")
        verdict = sem("verdict")
        verdict_pe = sem("verdict_pe")

        with nc.Block() as block:

            @block.sync
            def _(sp):
                for dst, src in ((wv[:, :], Wv), (w_nat[:, :], W), (acol[:, 0:1], a1_col),
                                 (acol[:, 1:2], a2_col), (bcol[:, :], b_col),
                                 (brow[:, :], b_row), (ba[:, :], ba_11)):
                    sp.dma_start(dst, src).then_inc(params_loaded, 16)
                for i in range(G // 2):
                    sp.dma_start(x_sb[:, 2 * Q * i:2 * Q * (i + 1), :],
                                 x_t[:, 2 * Q * i:2 * Q * (i + 1), :]).then_inc(x_loaded[i], 16)

                def load(g, c):
                    sp.dma_start(a_sb[:, :, c * CW:(c + 1) * CW],
                                 adj[bass.ds(g * GW, GW), c * CW:(c + 1) * CW]
                                 .rearrange("(q p) n -> p q n", p=P)).then_inc(a_loaded[c], 16)

                for c in range(CHUNKS):
                    load(0, c)
                sp.dma_start(diag[:, :], diagonal, allow_slow_non_contiguous=True).then_inc(diag_loaded, 16)

                def store(g):
                    sp.wait_ge(fin_step, FIN * (g + 1))
                    sp.dma_start(out_t[:, bass.ds(g * Q, Q), :], out_sb[:, :, :]).then_inc(stored, 16)

                def refill(g):
                    for c in range(CHUNKS):
                        sp.wait_ge(at_ready, PAIRS * (g - 1) + PPC * (c + 1))
                        sp.wait_ge(a_checked, CHUNKS * (g - 1) + c + 1)
                        load(g, c)

                refill(1)
                for g in range(2, G):
                    refill(g)
                    store(g - 2)
                for g in (G - 2, G - 1):
                    store(g)
                sp.wait_ge(stored, 16 * G)

            @block.gpsimd
            def _(pool):
                nc.gpsimd.memset(ident[:, :], 0.0).then_inc(consts_ready, 1)
                nc.gpsimd.memset(last_row[:, :], 0.0).then_inc(consts_ready, 1)
                nc.gpsimd.memset(e_last[:, :], 0.0).then_inc(consts_ready, 1)
                nc.gpsimd.memset(ones[:, :], 1.0).then_inc(consts_ready, 1)
                nc.gpsimd.memset(minus1[:, :], -1.0).then_inc(consts_ready, 1)
                nc.gpsimd.memset(minus_half[:, :], -0.5).then_inc(consts_ready, 1)
                pool.wait_ge(consts_ready, 6)
                nc.gpsimd.affine_select(out=ident[:, :], in_=ident[:, :], compare_op=ALU.not_equal, fill=1.0,
                                        base=0, pattern=[[-1, P]], channel_multiplier=1).then_inc(consts_ready, 1)
                nc.gpsimd.affine_select(out=last_row[:, :], in_=last_row[:, :], compare_op=ALU.not_equal, fill=-1.0,
                                        base=1 - P, pattern=[[0, P]], channel_multiplier=1).then_inc(consts_ready, 1)
                nc.gpsimd.memset(e_last[0:1, P - 1:P], 1.0).then_inc(consts_ready, 1)
                for i in range(G):
                    pool.wait_ge(norm0, 2 * i + 2)
                    if i >= 2:
                        pool.wait_ge(xhat_ready, i - 1)
                    nc.gpsimd.tensor_tensor(rstd[:, i % 2, :], rv[:, i % 2, :],
                                            minus_half[:, :].broadcast_to([P, Q]), ALU.pow).then_inc(rstd_ready, 1)
                with pool.Fori(0, G) as g:
                    pool.wait_ge(fin_step, FIN * g + FIN - 1)
                    nc.gpsimd.tensor_tensor(frstd[:, :], frv[:, :],
                                            minus_half[:, :].broadcast_to([P, Q]), ALU.pow).then_inc(rstd_ready, 1)

            @block.scalar
            def _(act):
                def square(i):
                    act.wait_ge(y0_ready, i + 1)
                    if i >= 2:
                        act.wait_ge(norm0, 2 * (i - 2) + 1)
                    nc.scalar.activation(sq[:, i % 2, :], bank[2 + i % 2][:, :], ACT.Square).then_inc(sq_ready, 1)

                def copy_s(i):
                    act.wait_ge(s_ready, i + 1)
                    nc.scalar.copy(s_all[:, i * GW:(i + 1) * GW], ps_den[:, :]).then_inc(s_copied, 1)

                for i in range(G + 4):
                    if i < G:
                        act.wait_ge(xt_ready, i + 1)
                        if i >= 2:
                            act.wait_ge(y0_ready, i - 1)
                        nc.scalar.copy(x_tr[:, i % 2, :], bank[i % 2][:, :]).then_inc(xt_copied, 1)
                    if 1 <= i <= G:
                        square(i - 1)
                    if i >= 4:
                        copy_s(i - 4)
                act.wait_ge(stat, BIASES)
                nc.scalar.activation(v_exp[:, :], st_cols[:, :, 1], ACT.Exp, bias=bias[:, 1:2],
                                     scale=SLOPE).then_inc(exps_ready, 1)
                nc.scalar.activation(w_exp[:, :], st_cols[:, :, 1], ACT.Exp, bias=bias[:, 0:1],
                                     scale=1 - SLOPE).then_inc(exps_ready, 1)
                act.wait_ge(s_copied, G)

                def row_exps(g):
                    nc.scalar.activation(R[:, :], s_all[:, bass.ds(g * GW, GW)], ACT.Exp, bias=bias[:, 3:4],
                                         scale=1 - SLOPE).then_inc(exps_ready, 1)

                row_exps(0)

                def check_values(g, c, first):
                    act.wait_ge(a_loaded[c], 16 * (g + 1))
                    if not (first and c == 0):
                        act.wait_ge(a_checked, CHUNKS * g + c)
                    nc.scalar.activation(a_junk[:, :].rearrange("p (q n) -> p q n", q=Q), a_sb[:, :, c * CW:(c + 1) * CW],
                                         ACT.Square, bias=minus_half[:, :],
                                         accum_out=a_sum[:, bass.ds(g * CHUNKS + c, 1)]).then_inc(a_checked, 1)

                def group(g, first=False, last=False):
                    act.wait_ge(exps_ready, g + 3)
                    for p in range(PAIRS):
                        if not (first and p < NE):
                            act.wait_ge(mm_done, PAIRS * g + p - NE + 1)
                        for half in range(2):
                            ins = nc.scalar.activation(e_sb[:, p % NE, half * GW:(half + 1) * GW],
                                                       R[:, :], ACT.Relu, bias=minus1[:, :],
                                                       scale=w_exp[:, 2 * p + half:2 * p + half + 1])
                        ins.then_inc(e_ready, 1)
                        if p % PPC == PPC - 1:
                            check_values(g, p // PPC, first)
                        if p == NE - 2 and not first:
                            act.wait_ge(mm_done, PAIRS * g)
                            copy_acc()
                    if not last:
                        act.wait_ge(e_ready, PAIRS * (g + 1))
                        row_exps(g + 1)

                def copy_acc():
                    nc.scalar.copy(acc_t[:, :], ps_acc[:, :]).then_inc(acc_copied, 1)

                group(0, first=True)
                with act.Fori(1, G - 1) as g:
                    group(g)
                group(G - 1, last=True)
                act.wait_ge(mm_done, PAIRS * G)
                copy_acc()

            @block.vector
            def _(dve):
                done = [0]

                def step(ins, s=vec_const):
                    done[0] += 1
                    ins.then_inc(s, 1)
                    dve.wait_ge(s, done[0])

                def centre(dst, src, c):
                    step(nc.vector.reduce_sum(mean[:, c:c + 1], src, AX))
                    step(nc.vector.tensor_scalar(mean[:, c + 1:c + 2], mean[:, c:c + 1], 1.0 / D, None, ALU.mult))
                    step(nc.vector.tensor_scalar(dst, src, mean[:, c + 1:c + 2], None, ALU.subtract))

                dve.wait_ge(consts_ready, 9)
                dve.wait_ge(params_loaded, 16 * 7)
                step(nc.vector.tensor_tensor(m0[:, :], wv[:, :], ident[:, :], ALU.add))
                centre(m0c[:, :], m0[:, :], 0)
                assert done[0] == M0_READY
                step(nc.vector.tensor_copy(ident16[:, :], ident[:, :]))
                step(nc.vector.tensor_tensor(less_last[:, :], ident[:, :], last_row[:, :], ALU.add))
                step(nc.vector.tensor_tensor(bb[:, :], acol[:, 0:1], acol[:, 1:2], ALU.add))
                step(nc.vector.tensor_tensor(bb[:, :], bb[:, :], bcol[:, :], ALU.mult))
                dve.wait_ge(pe_const, 1)
                step(nc.vector.tensor_copy(w_t[:, :], ps_misc[:, 0:D]))
                step(nc.vector.tensor_copy(u[:, :], ps_misc[:, D:D + 2]))
                step(nc.vector.tensor_scalar(u1_rep[:, :], ones[:, :], u[:, 0:1], None, ALU.mult))
                assert done[0] == U_READY
                dve.wait_ge(pe_const, 2)
                step(nc.vector.tensor_copy(cs[:, :], ps_misc[:, D + 2:D + 3]))
                step(nc.vector.tensor_copy(w2[:, :], ps_misc[:, 2 * D:3 * D]))
                centre(w2c[:, :], w2[:, :], 2)
                assert done[0] == W2_READY

                def variance(i):
                    k = i % 2
                    dve.wait_ge(sq_ready, i + 1)
                    if i >= 2:
                        dve.wait_ge(rstd_ready, i - 1)
                    nc.vector.reduce_sum(ss[:, k, :], sq[:, k, :].rearrange("p (q d) -> p q d", q=Q),
                                         AX).then_inc(norm0, 1)
                    dve.wait_ge(norm0, 2 * i + 1)
                    nc.vector.tensor_scalar(rv[:, k, :], ss[:, k, :], 1.0 / D, EPS, ALU.mult,
                                            ALU.add).then_inc(norm0, 1)

                def divide(i):
                    k = i % 2
                    dve.wait_ge(rstd_ready, i + 1)
                    nc.vector.tensor_tensor(xhat[:, Q * i:Q * (i + 1), :],
                                            bank[2 + k][:, :].rearrange("p (q d) -> p q d", q=Q),
                                            rstd[:, k, :].unsqueeze(2).broadcast_to([P, Q, D]),
                                            ALU.mult).then_inc(xhat_ready, 1)

                for i in range(G + 2):
                    if i < G:
                        variance(i)
                    if 1 <= i <= G:
                        divide(i - 1)
                    if i >= 2:
                        dve.wait_ge(xht_ready, i - 1)
                        nc.vector.tensor_copy(xhat_t[:, (i - 2) * GW:(i - 1) * GW],
                                              bank[4 + i % 2][:, :]).then_inc(xht_copied, 1)

                done[0] = 0
                dve.wait_ge(s_ready, G)
                step(nc.vector.tensor_copy(st_cols[:, :, :].rearrange("p t c -> p (t c)"),
                                           ps_misc[:, 3 * D:3 * D + 2 * T]), stat)
                for c, (col, op) in enumerate(((1, ALU.max), (1, ALU.min), (0, ALU.max), (0, ALU.min))):
                    nc.vector.tensor_reduce(ext[:, c:c + 1], st_cols[:, :, col], AX, op).then_inc(stat, 1)
                done[0] += 4
                dve.wait_ge(stat, done[0])
                step(nc.vector.tensor_scalar(ext[:, 1::2], ext[:, 1::2], -1.0, None, ALU.mult), stat)
                assert done[0] == EXT_READY
                dve.wait_ge(stat_pe, 1)
                step(nc.vector.reduce_max(ext_max[:, :], ps_misc[0:4, 0:P], AX), stat)
                step(nc.vector.tensor_scalar(ext_diag[:, :], ident[0:4, 0:4], ext_max[:, :], None, ALU.mult), stat)
                assert done[0] == DIAG_READY
                dve.wait_ge(stat_pe, 2)
                step(nc.vector.tensor_copy(ext_all[:, :], ps_misc[:, D:D + 4]), stat)
                nc.vector.tensor_scalar(bias[:, 0:1], ext_all[:, 0:1], SLOPE - 1, None, ALU.mult).then_inc(stat, 1)
                nc.vector.tensor_scalar(bias[:, 1:2], ext_all[:, 0:1], -SLOPE, None, ALU.mult).then_inc(stat, 1)
                nc.vector.tensor_tensor(bias[:, 2:3], ext_all[:, 0:1], cs[:, :], ALU.add).then_inc(stat, 1)
                done[0] += 3
                dve.wait_ge(stat, done[0])
                step(nc.vector.tensor_scalar(bias[:, 3:4], bias[:, 2:3], 1 - SLOPE, None, ALU.mult), stat)
                assert done[0] == BIASES

                dve.wait_ge(exps_ready, 1)
                for n in range(T // FT):
                    ts = slice(FT * n, FT * (n + 1))
                    nc.vector.tensor_tensor(feat[:, ts, 0:D - 1], xhat[:, ts, 0:D - 1],
                                            v_exp[:, ts].unsqueeze(2).broadcast_to([P, FT, D - 1]),
                                            ALU.mult).then_inc(feat_ready, 1)
                    nc.vector.tensor_copy(feat[:, ts, D - 1], v_exp[:, ts]).then_inc(feat_ready, 1)

                def finish(g, n, first=False):
                    o = ps_out[:, :].rearrange("p (q d) -> p q d", q=Q)
                    if n == 0:
                        dve.wait_ge(fin_mm, g + 1)
                    else:
                        dve.wait_ge(fin_step, FIN * g + n)
                    if n == 0:
                        ins = nc.vector.reciprocal(rden[:, :], ps_den[:, 0:Q])
                    elif n == 1:
                        ins = nc.vector.tensor_tensor(y[:, :, :], o, rden[:, :].unsqueeze(2).broadcast_to([P, Q, D]),
                                                      ALU.mult)
                    elif n == 2:
                        ins = nc.vector.tensor_tensor(y[:, :, :], y[:, :, :], xhat[:, bass.ds(g * Q, Q), :], ALU.add)
                    elif n == 3:
                        ins = nc.vector.tensor_tensor(ysq[:, :, :], y[:, :, :], y[:, :, :], ALU.mult)
                    elif n == 4:
                        ins = nc.vector.reduce_sum(fss[:, :], ysq[:, :, :], AX)
                    elif n == 5:
                        ins = nc.vector.tensor_scalar(frv[:, :], fss[:, :], 1.0 / D, EPS, ALU.mult, ALU.add)
                    else:
                        dve.wait_ge(rstd_ready, G + g + 1)
                        if not first:
                            dve.wait_ge(stored, 16 * g)
                        ins = nc.vector.tensor_tensor(out_sb[:, :, :], y[:, :, :],
                                                      frstd[:, :].unsqueeze(2).broadcast_to([P, Q, D]), ALU.mult)
                    ins.then_inc(fin_step, 1)

                def group(g, first=False, second=False):
                    for p in range(PAIRS):
                        dve.wait_ge(at_ready, PAIRS * g + p + 1)
                        dve.wait_ge(e_ready, PAIRS * g + p + 1)
                        e = e_sb[:, p % NE, :]
                        nc.vector.scalar_tensor_tensor(out=e, in0=e, scalar=1.0, in1=ps_at_int[p % NA],
                                                       op0=ALU.add, op1=ALU.mult).then_inc(p_ready, 1)
                        if not first and 6 <= p < 12:
                            finish(g - 1, p - 6, first=second)
                        if not first and p == 13:
                            finish(g - 1, FIN - 1, first=second)

                group(0, first=True)
                group(1, second=True)
                with dve.Fori(2, G) as g:
                    group(g)
                for n in range(FIN):
                    finish(G - 1, n)

                done[0] = 0
                dve.wait_ge(a_checked, G * CHUNKS)
                dve.wait_ge(diag_loaded, 16)
                step(nc.vector.reduce_max(checks[:, 0:1], a_sum[:, :], AX), verdict)
                step(nc.vector.tensor_scalar(checks[:, 0:1], checks[:, 0:1], Q * CW / 4.0, None, ALU.is_le), verdict)
                step(nc.vector.tensor_reduce(checks[:, 1:2], diag[:, :], AX, ALU.min), verdict)
                step(nc.vector.tensor_scalar(checks[:, 1:2], checks[:, 1:2], 1.0, None, ALU.is_ge), verdict)
                step(nc.vector.tensor_tensor(checks[:, 2:3], ext_all[:, 0:1], ext_all[:, 1:2], ALU.add), verdict)
                step(nc.vector.tensor_tensor(checks[:, 3:4], ext_all[:, 2:3], bias[:, 2:3], ALU.add), verdict)
                step(nc.vector.tensor_tensor(checks[:, 4:5], ext_all[:, 3:4], bias[:, 2:3], ALU.subtract), verdict)
                step(nc.vector.tensor_scalar(checks[:, 2:5], checks[:, 2:5], LIMIT, None, ALU.is_le), verdict)
                step(nc.vector.reduce_sum(bad_cols[:, :], checks[:, :], AX), verdict)
                assert done[0] == CHECKS_READY
                dve.wait_ge(verdict_pe, 1)
                total = float(5 * P)
                if force_general:
                    total += 1.0
                step(nc.vector.tensor_scalar(flag[:, :], ps_misc[0:1, 0:1], total, None, ALU.not_equal), verdict)

            @block.tensor
            def _(pe):
                pe.wait_ge(consts_ready, 9)
                pe.wait_ge(params_loaded, 16 * 7)

                def transposes(dst, src):
                    for q in range(Q):
                        ins = nc.tensor.transpose(dst[:, q * P:(q + 1) * P], src(q), ident[:, :])
                    return ins

                def x_transposed(i):
                    pe.wait_ge(x_loaded[i // 2], 16)
                    if i >= 2:
                        pe.wait_ge(xt_copied, i - 1)
                    transposes(bank[i % 2], lambda q: x_sb[:, Q * i + q, :]).then_inc(xt_ready, 1)

                def layer0(i):
                    pe.wait_ge(xt_copied, i + 1)
                    if i >= 2:
                        pe.wait_ge(xhat_ready, i - 1)
                    for q in range(Q):
                        ins = nc.tensor.matmul(bank[2 + i % 2][:, q * P:(q + 1) * P],
                                               x_tr[:, i % 2, q * P:(q + 1) * P], m0c[:, :], start=True, stop=True)
                    ins.then_inc(y0_ready, 1)

                def xhat_transposed(i):
                    pe.wait_ge(xhat_ready, i + 1)
                    if i >= 2:
                        pe.wait_ge(xht_copied, i - 1)
                    transposes(bank[4 + i % 2], lambda q: xhat[:, Q * i + q, :]).then_inc(xht_ready, 1)

                def scores(i):
                    pe.wait_ge(xht_copied, i + 1)
                    if i >= 1:
                        pe.wait_ge(s_copied, i)
                    for q in range(Q):
                        t = Q * i + q
                        nc.tensor.matmul(ps_misc[:, 3 * D + 2 * t:3 * D + 2 * t + 2],
                                         xhat_t[:, t * P:(t + 1) * P], u[:, :], start=True, stop=True)
                    nc.tensor.matmul(ps_den[:, :], u1_rep[:, :], xhat_t[:, i * GW:(i + 1) * GW],
                                     start=True, stop=True).then_inc(s_ready, 1)

                x_transposed(0)
                nc.tensor.transpose(ps_misc[:, 0:D], w_nat[:, :], ident[:, :])
                nc.tensor.matmul(ps_misc[:, D:D + 2], w_nat[:, :], acol[:, :], start=True,
                                 stop=True).then_inc(pe_const, 1)
                pe.wait_ge(vec_const, M0_READY)
                x_transposed(1)
                layer0(0)
                pe.wait_ge(vec_const, U_READY)
                nc.tensor.matmul(ps_misc[:, D + 2:D + 3], ones[:, :], bb[:, :], start=True, stop=False)
                nc.tensor.matmul(ps_misc[:, D + 2:D + 3], ones[0:1, :], ba[:, :], start=False, stop=True)
                nc.tensor.matmul(ps_misc[:, 2 * D:3 * D], less_last[:, :], w_t[:, :], start=True, stop=False)
                nc.tensor.matmul(ps_misc[:, 2 * D:3 * D], e_last[:, :], brow[:, :], start=False,
                                 stop=True).then_inc(pe_const, 1)
                pe.wait_ge(vec_const, W2_READY)
                for i in range(2, G + 5):
                    if i < G:
                        x_transposed(i)
                    if i - 1 < G:
                        layer0(i - 1)
                    if 0 <= i - 3 < G:
                        xhat_transposed(i - 3)
                    if 0 <= i - 4 < G:
                        scores(i - 4)
                pe.wait_ge(stat, EXT_READY)
                nc.tensor.transpose(ps_misc[0:4, 0:P], ext[:, :], ident[:, :]).then_inc(stat_pe, 1)
                pe.wait_ge(stat, DIAG_READY)
                nc.tensor.matmul(ps_misc[:, D:D + 4], ones[0:4, :], ext_diag[:, :], start=True,
                                 stop=True).then_inc(stat_pe, 1)
                pe.wait_ge(xhat_ready, G)
                pe.wait_ge(xht_copied, G)
                pe.wait_ge(s_copied, G)

                half_words = a_sb[:, :, :].rearrange("p q n -> p (q n)").bitcast(F16).rearrange(
                    "p (q n two) -> p q n two", q=Q, two=2)[:, :, :, 0]

                def pair(g, p, early=False):
                    if p % PPC == 0:
                        pe.wait_ge(a_loaded[p // PPC], 16 * (g + 1))
                    if not early:
                        pe.wait_ge(p_ready, PAIRS * g + p - NA + 1)
                    for half in range(2):
                        for q in range(Q):
                            j = (2 * p + half) * P
                            c = half * GW + q * P
                            ins = nc.tensor.transpose(ps_at[p % NA][:, c:c + P], half_words[:, q, j:j + P],
                                                      ident16[:, :])
                    ins.then_inc(at_ready, 1)

                def sums(g, p, first):
                    if p == 0 and not first:
                        pe.wait_ge(acc_copied, g)
                    if first and (2 * p) % FT == 0:
                        pe.wait_ge(feat_ready, 2 * (2 * p // FT + 1))
                    pe.wait_ge(p_ready, PAIRS * g + p + 1)
                    for half in range(2):
                        j = 2 * p + half
                        ins = nc.tensor.matmul(ps_acc[:, :], feat[:, j, :], e_sb[:, p % NE, half * GW:(half + 1) * GW],
                                               start=(j == 0), stop=(j == T - 1))
                    ins.then_inc(mm_done, 1)

                def project(g, first=False):
                    pe.wait_ge(acc_copied, g + 1)
                    if not first:
                        pe.wait_ge(fin_step, FIN * (g - 1) + 2)
                    for q in range(Q):
                        nc.tensor.matmul(ps_den[:, q:q + 1], acc_t[:, q * P:(q + 1) * P], ident[:, P - 1:P],
                                         start=True, stop=True)
                    for q in range(Q):
                        ins = nc.tensor.matmul(ps_out[:, q * P:(q + 1) * P], acc_t[:, q * P:(q + 1) * P], w2c[:, :],
                                               start=True, stop=True)
                    ins.then_inc(fin_mm, 1)

                def group(g, first=False, second=False, last=False):
                    for p in range(PAIRS):
                        n = p + AHEAD
                        if n < PAIRS:
                            pair(g, n, early=first and n < NA)
                        elif not last:
                            pair(g + 1, n - PAIRS)
                        sums(g, p, first)
                        if p == 4 and not first:
                            project(g - 1, first=second)

                for p in range(AHEAD):
                    pair(0, p, early=True)
                group(0, first=True)
                group(1, second=True)
                with pe.Fori(2, G - 1) as g:
                    group(g)
                group(G - 1, last=True)
                project(G - 1)

                pe.wait_ge(verdict, CHECKS_READY)
                nc.tensor.matmul(ps_misc[0:1, 0:1], bad_cols[:, :], ones[:, 0:1], start=True,
                                 stop=True).then_inc(verdict_pe, 1)

        wq = sb("wq", [P, D])
        wk = sb("wk", [P, D])
        q_cur = sb("q_cur", [P, P])
        u2_rep = sb("u2_rep", [P, P])
        s_cur = sb("s_cur", [P, 1])
        s_col = sb("s_col", [P, T])
        neg_max = sb("neg_max", [P, 1])
        row_sum = sb("row_sum", [P, 1])
        a_row = a_sb[:, 0, :]
        scores_row = a_sb[:, 1, :].bitcast(F32)
        k_t = a_sb[:, 2, :].bitcast(F32)
        q_t = a_sb[:, 3, :].bitcast(F32)
        mask = s_all[:, :]
        p_t = e_sb[:, :, :].rearrange("p n c -> p (n c)")
        values = feat
        yg, yg2 = y[:, 0, :], y[:, 1, :]

        g_loaded = sem("g_loaded")
        g_made = sem("g_made")
        g_kept = sem("g_kept")
        g_small = sem("g_small")
        g_adj = [sem(f"g_adj{n}") for n in range(2)]
        g_query = [sem(f"g_query{n}") for n in range(2)]
        g_prod = [sem(f"g_prod{n}") for n in range(2)]
        g_vec = [sem(f"g_vec{n}") for n in range(2)]
        g_exp = [sem(f"g_exp{n}") for n in range(2)]
        g_pt = [sem(f"g_pt{n}") for n in range(2)]
        g_pt_kept = [sem(f"g_pt_kept{n}") for n in range(2)]
        g_sums = [sem(f"g_sums{n}") for n in range(2)]
        g_rstd = [sem(f"g_rstd{n}") for n in range(2)]
        g_stored = sem("g_stored")
        KEPT = [4 * G, 7 * G]
        SCORED = [16, 10]
        VARIED = [25, 19]
        ROWS = [26, 20]

        def if_general(eng):
            return eng.If(eng.value_load(flag[0:1, 0:1]) != 0)

        with nc.Block() as block:

            @block.tensor
            def _(pe):
                with if_general(pe):
                    made = [0]

                    def product(ins):
                        made[0] += 1
                        ins.then_inc(g_made, 1)
                        pe.wait_ge(g_kept, made[0])

                    def turned(src):
                        for i in range(G):
                            for q in range(Q):
                                ins = nc.tensor.transpose(bank[0][:, q * P:(q + 1) * P], src[:, Q * i + q, :],
                                                          ident[:, :])
                            product(ins)

                    def by_rows(w):
                        for i in range(G):
                            product(nc.tensor.matmul(bank[0][:, :], w[:, :], xhat_t[:, i * GW:(i + 1) * GW],
                                                     start=True, stop=True))

                    def by_cols(w, bias_row):
                        for i in range(G):
                            for q in range(Q):
                                t = Q * i + q
                                dst = bank[0][:, q * P:(q + 1) * P]
                                ins = nc.tensor.matmul(dst, xhat_t[:, t * P:(t + 1) * P], w[:, :], start=True,
                                                       stop=bias_row is None)
                                if bias_row is not None:
                                    ins = nc.tensor.matmul(dst, ones[0:1, :], bias_row[:, :], start=False, stop=True)
                            product(ins)

                    def tiles(n):
                        with pe.Fori(0, T) as t:
                            if n == 0:
                                pe.wait_ge(g_query[n], t + 1)
                                for c in range(G):
                                    nc.tensor.matmul(bank[c][:, :], q_cur[:, :], k_t[:, c * GW:(c + 1) * GW],
                                                     start=True, stop=True).then_inc(g_prod[n], 1)
                            pe.wait_ge(g_exp[n], t + 1)
                            for c in range(G):
                                for q in range(Q):
                                    j = Q * c + q
                                    ins = nc.tensor.transpose(bank[c][:, q * P:(q + 1) * P],
                                                              scores_row[:, j * P:(j + 1) * P], ident[:, :])
                                ins.then_inc(g_pt[n], 1)
                            pe.wait_ge(g_pt_kept[n], G * (t + 1))
                            for j in range(T):
                                ins = nc.tensor.matmul(bank[0][:, 0:D], p_t[:, j * P:(j + 1) * P], values[:, j, :],
                                                       start=(j == 0), stop=(j == T - 1))
                            ins.then_inc(g_sums[n], 1)
                            pe.wait_ge(g_vec[n], ROWS[n] * (t + 1))

                    pe.wait_ge(g_loaded, 32)
                    turned(x_sb)
                    by_rows(wq)
                    by_rows(wk)
                    by_cols(wv, None)
                    tiles(0)
                    turned(xhat)
                    pe.wait_ge(g_small, 1)
                    by_rows(u2_rep)
                    by_cols(w_t, brow)
                    assert made[0] == KEPT[1]
                    for t in range(T):
                        ins = nc.tensor.matmul(bank[1][:, t:t + 1], xhat_t[:, t * P:(t + 1) * P], u[:, 0:1],
                                               start=True, stop=True)
                    ins.then_inc(g_made, 1)
                    tiles(1)

            @block.scalar
            def _(act):
                with if_general(act):
                    kept = [0]

                    def keep(dst):
                        kept[0] += 1
                        act.wait_ge(g_made, kept[0])
                        nc.scalar.copy(dst, bank[0][:, :]).then_inc(g_kept, 1)

                    def keep_all(dst):
                        for i in range(G):
                            keep(dst(i))

                    def cols(buf):
                        return lambda i: buf[:, i * GW:(i + 1) * GW]

                    def by_tile(buf):
                        return lambda i: buf[:, Q * i:Q * (i + 1), :].rearrange("p q d -> p (q d)")

                    def tiles(n):
                        with act.Fori(0, T) as t:
                            act.dma_start(a_row, adj[bass.ds(t * P, P), :]).then_inc(g_adj[n], 16)
                            act.wait_ge(g_vec[n], ROWS[n] * t + SCORED[n])
                            nc.scalar.activation(scores_row, scores_row, ACT.Exp,
                                                 accum_out=row_sum[:, :]).then_inc(g_exp[n], 1)
                            for c in range(G):
                                act.wait_ge(g_pt[n], G * t + c + 1)
                                nc.scalar.copy(p_t[:, c * GW:(c + 1) * GW], bank[c][:, :]).then_inc(g_pt_kept[n], 1)
                            act.wait_ge(g_vec[n], ROWS[n] * (t + 1))
                            if n == 1:
                                act.dma_start(out_t[:, bass.ds(t, 1), :], out_sb[:, 0:1, :]).then_inc(g_stored, 16)
                                act.wait_ge(g_stored, 16 * (t + 1))

                    keep_all(cols(xhat_t))
                    keep_all(cols(q_t))
                    keep_all(cols(k_t))
                    keep_all(by_tile(values))
                    assert kept[0] == KEPT[0]
                    tiles(0)
                    keep_all(cols(xhat_t))
                    keep_all(cols(k_t))
                    keep_all(by_tile(values))
                    tiles(1)

            @block.sync
            def _(sp):
                with if_general(sp):
                    sp.dma_start(wq[:, :], Wq).then_inc(g_loaded, 16)
                    sp.dma_start(wk[:, :], Wk).then_inc(g_loaded, 16)
                    sp.wait_ge(g_loaded, 32)

            @block.gpsimd
            def _(pool):
                with if_general(pool):
                    for n in range(2):
                        with pool.Fori(0, T) as t:
                            pool.wait_ge(g_vec[n], ROWS[n] * t + VARIED[n])
                            nc.gpsimd.tensor_tensor(frstd[:, 0:1], frv[:, 0:1], minus_half[:, :],
                                                    ALU.pow).then_inc(g_rstd[n], 1)

            @block.vector
            def _(dve):
                with if_general(dve):
                    def tiles(n):
                        dve.wait_ge(g_kept, KEPT[n])
                        with dve.Fori(0, T) as t:
                            done = [0]

                            def step(ins):
                                done[0] += 1
                                ins.then_inc(g_vec[n], 1)
                                dve.wait_ge(g_vec[n], ROWS[n] * t + done[0])

                            if n == 0:
                                step(nc.vector.tensor_copy(q_cur[:, :], q_t[:, bass.ds(t * P, P)]))
                                dve.sem_inc(g_query[n], 1)
                                dve.wait_ge(g_adj[n], 16 * (t + 1))
                                step(nc.vector.tensor_copy(mask, a_row))
                                own = s_all[:, bass.ds(t * P, P)]
                                step(nc.vector.tensor_tensor(own, own, ident[:, :], ALU.add))
                                step(nc.vector.tensor_scalar(mask, mask, -1.0, -1.0, ALU.add, ALU.max))
                                step(nc.vector.tensor_scalar(mask, mask, 1.0, FLT_MAX, ALU.min, ALU.mult))
                                for c in range(G):
                                    dve.wait_ge(g_prod[n], G * t + c + 1)
                                    cc = slice(c * GW, (c + 1) * GW)
                                    step(nc.vector.tensor_tensor(scores_row[:, cc], bank[c][:, :], mask[:, cc],
                                                                 ALU.add))
                            else:
                                step(nc.vector.tensor_copy(s_cur[:, :], s_col[:, bass.ds(t, 1)]))
                                step(nc.vector.tensor_scalar(scores_row, k_t, s_cur[:, :], None, ALU.add))
                                step(nc.vector.scalar_tensor_tensor(out=scores_row, in0=scores_row, scalar=SLOPE,
                                                                    in1=scores_row, op0=ALU.mult, op1=ALU.max))
                                dve.wait_ge(g_adj[n], 16 * (t + 1))
                                step(nc.vector.tensor_scalar(mask, a_row, 0.0, None, ALU.is_gt))
                                step(nc.vector.tensor_tensor(scores_row, scores_row, mask, ALU.mult))
                                step(nc.vector.tensor_scalar(mask, mask, -1.0, NEG, ALU.add, ALU.mult))
                                step(nc.vector.tensor_tensor(scores_row, scores_row, mask, ALU.add))
                            step(nc.vector.reduce_max(neg_max[:, :], scores_row, AX))
                            step(nc.vector.tensor_scalar(neg_max[:, :], neg_max[:, :], -1.0, None, ALU.mult))
                            step(nc.vector.tensor_scalar(scores_row, scores_row, neg_max[:, :], -FLT_MAX, ALU.add,
                                                         ALU.max))
                            assert done[0] == SCORED[n]
                            dve.wait_ge(g_sums[n], t + 1)
                            step(nc.vector.reciprocal(rden[:, 0:1], row_sum[:, :]))
                            step(nc.vector.tensor_scalar(yg, bank[0][:, 0:D], rden[:, 0:1], None, ALU.mult))
                            x_in = x_sb if n == 0 else xhat
                            step(nc.vector.tensor_tensor(y[:, 0:1, :], y[:, 0:1, :], x_in[:, bass.ds(t, 1), :],
                                                         ALU.add))
                            step(nc.vector.reduce_sum(mean[:, 0:1], yg, AX))
                            step(nc.vector.tensor_scalar(mean[:, 1:2], mean[:, 0:1], 1.0 / D, None, ALU.mult))
                            step(nc.vector.tensor_scalar(yg, yg, mean[:, 1:2], None, ALU.subtract))
                            step(nc.vector.tensor_tensor(yg2, yg, yg, ALU.mult))
                            step(nc.vector.reduce_sum(fss[:, 0:1], yg2, AX))
                            step(nc.vector.tensor_scalar(frv[:, 0:1], fss[:, 0:1], 1.0 / D, EPS, ALU.mult, ALU.add))
                            assert done[0] == VARIED[n]
                            dve.wait_ge(g_rstd[n], t + 1)
                            dst = xhat[:, bass.ds(t, 1), :] if n == 0 else out_sb[:, 0:1, :]
                            step(nc.vector.tensor_scalar(dst, y[:, 0:1, :], frstd[:, 0:1], None, ALU.mult))
                            assert done[0] == ROWS[n]

                    tiles(0)
                    nc.vector.tensor_scalar(u2_rep[:, :], ones[:, :], u[:, 1:2], None, ALU.mult).then_inc(g_small, 1)
                    dve.wait_ge(g_kept, KEPT[1])
                    dve.wait_ge(g_made, KEPT[1] + 1)
                    nc.vector.tensor_scalar(s_col[:, :], bank[1][:, 0:T], cs[:, :], None,
                                            ALU.add).then_inc(g_small, 1)
                    dve.wait_ge(g_small, 2)
                    tiles(1)


_INS = ['x', 'adj', 'L0_gnn_Wq', 'L0_gnn_Wk', 'L0_gnn_Wv', 'L1_gnn_W', 'L1_gnn_b_W', 'L1_gnn_a_vec', 'L1_gnn_b_a']


def kernel(**inputs):
    import numpy as _np
    import concourse.bacc as _bacc
    from concourse import mybir as _mybir
    from concourse.bass_utils import run_bass_kernel_spmd as _run

    nc = _bacc.Bacc("TRN2", target_bir_lowering=False, num_devices=1)
    arrays, args = {}, []
    for name in _INS:
        a = _np.ascontiguousarray(inputs[name])
        arrays[f"in_{name}_dram"] = a
        args.append(nc.dram_tensor(f"in_{name}_dram", a.shape, _mybir.dt.from_np(a.dtype), kind="ExternalInput").ap())
    out = nc.dram_tensor("out_0_dram", inputs["x"].shape, _mybir.dt.float32, kind="ExternalOutput").ap()
    graph_layers(nc, args[0], args[1], args[2], args[3], args[4], args[5], args[6], args[7], args[8], out)
    r = _run(nc, [arrays], core_ids=[0])
    return r.results[0]["out_0_dram"]
```

```python
from contextlib import ExitStack

import numpy as np
import concourse.bass as bass
from concourse import mybir

F32 = mybir.dt.float32
F16 = mybir.dt.float16
I32 = mybir.dt.int32
U32 = mybir.dt.uint32
U16 = mybir.dt.uint16
ALU = mybir.AluOpType
ACT = mybir.ActivationFunctionType
AX = mybir.AxisListType.X
AXY = mybir.AxisListType.XY

P = 128
EPS = 1e-5
SLOPE = 0.2
LIMIT = 60.0
FLT_MIN = float(np.finfo(np.float32).tiny)
FLT_MAX = float(np.finfo(np.float32).max)
NEG = 9e15


def graph_layers(nc, x, adj, Wq, Wk, Wv, W, b, a_vec, b_a, out, force_general=False):
    N, D = x.shape
    assert D == P and N % 512 == 0
    T = N // P
    Q = 4
    GW = Q * P
    G = N // GW
    PAIRS = T // 2
    CHUNKS = 4
    CW = N // CHUNKS
    PPC = PAIRS // CHUNKS
    NA = 4
    NE = 8
    AHEAD = 2
    assert PAIRS % NA == 0 and PAIRS % NE == 0 and PPC == Q
    FIN = 8
    BY_VECTOR = [0, 2, 4, 6, 8]
    BY_SCALAR = [p for p in range(PAIRS) if p not in BY_VECTOR]
    N_VEC, N_ACT = len(BY_VECTOR), len(BY_SCALAR)
    COPY_AT, PROJECT_AT, FIN_AT = 3, 3, 6
    DIAG_AT, SPREAD_AT = 5, 10
    FIRST_SLOT = TURN = -12
    COPY = -11
    MULTIPLY = -10
    KEEP = -8
    SQUARE = -8
    VARY = -7
    DIVIDE = -6
    SPREAD0_AT = -5
    EXPS = FEATURES = -4
    X_FIRST = 6
    M0_READY, U_READY, M0T_READY, CS_READY = 5, 9, 11, 13
    W2_READ, BIASES = 14, 22
    CHECKS_READY = 12

    x_t = x.rearrange("(t p) d -> p t d", p=P)
    out_t = out.rearrange("(t p) d -> p t d", p=P)
    a1_col = a_vec[0:D].rearrange("(p c) -> p c", c=1)
    a2_col = a_vec[D:2 * D].rearrange("(p c) -> p c", c=1)
    b_col = b.rearrange("(p c) -> p c", c=1)
    b_row = b.rearrange("(a d) -> a d", a=1)
    diagonal = adj.rearrange("i j -> (i j)")[0:N * N:N + 1].rearrange("(t p) -> p t", p=P)
    ba_11 = b_a.rearrange("(a d) -> a d", a=1)

    with ExitStack() as ctx:
        def sb(name, shape, dt=F32):
            return ctx.enter_context(nc.sbuf_tensor(name, shape, dt))

        def sem(name):
            return ctx.enter_context(nc.semaphore(name))

        banks = ctx.enter_context(nc.psum_tensor("banks", [P, 8, 512], F32))
        bank = [banks[:, i, :] for i in range(8)]
        ps_at = [bank[i][:, :].bitcast(F16) for i in range(NA)]
        ps_at_int = [bank[i][:, :].bitcast(U16) for i in range(NA)]
        ps_w2 = bank[4]
        ps_acc = [bank[4], bank[5]]
        ps_xt = bank[5]
        ps_quad = banks[:, 6:8, :].rearrange("p b (h c) -> p (b h) c", h=2)
        ps_row = bank[6]
        ps_misc = bank[7]

        ident = sb("ident", [P, P])
        ones = sb("ones", [P, P])
        wv = sb("wv", [P, D])
        w_nat = sb("w_nat", [P, D])
        w_t = sb("w_t", [P, D])
        acol = sb("acol", [P, 2])
        bcol = sb("bcol", [P, 1])
        brow = sb("brow", [1, D])
        ba = sb("ba", [1, 1])
        u = sb("u", [P, 2])
        bb = sb("bb", [P, 2])
        cs = sb("cs", [P, 2])
        flag = sb("flag", [1, 1], I32)
        a_sb = sb("a_sb", [P, Q, N], I32)
        x_sb = sb("x_sb", [P, T, D])
        xhat_st = sb("xhat_st", [P, T, D + 2])
        xhat, st_cols = xhat_st[:, :, 0:D], xhat_st[:, :, D:D + 2]
        feat = sb("feat", [P, T, D])
        R = sb("R", [P, GW])
        e_sb = sb("e_sb", [P, NE, 2 * GW])
        x_tr = sb("x_tr", [P, 2, GW])
        sq = sb("sq", [P, 2, GW])
        last_row = sb("last_row", [P, P])
        less_last = sb("less_last", [P, P])
        e_last = sb("e_last", [1, P])
        ident16 = sb("ident16", [P, P], F16)
        m0 = sb("m0", [P, D])
        m0c_um = sb("m0c_um", [P, D + 2])
        m0c = m0c_um[:, 0:D]
        um = m0c_um[:, D:D + 2]
        m0c_t = sb("m0c_t", [P, D])
        w2 = sb("w2", [P, D])
        w2c_den = sb("w2c_den", [P, D + 1])
        w2c = w2c_den[:, 0:D]
        pick_den = w2c_den[:, D:D + 1]
        mean = sb("mean", [P, 4])
        ss = sb("ss", [P, 2, Q])
        rv = sb("rv", [P, 2, Q])
        rstd = sb("rstd", [P, 2, Q])
        s_diag = sb("s_diag", [P, Q, P])
        norm_u = sb("norm_u", [P, 1])
        bias = sb("bias", [P, 4])
        minus1 = sb("minus1", [P, 1])
        minus_half = sb("minus_half", [P, 1])
        half = sb("half", [P, 1])
        w_exp = sb("w_exp", [P, T])
        v_exp = sb("v_exp", [P, T])
        acc_t = sb("acc_t", [P, GW])
        y = sb("y", [P, Q, D])
        ysq = sb("ysq", [P, Q, D])
        den = sb("den", [P, Q])
        rden = sb("rden", [P, Q])
        fss = sb("fss", [P, Q])
        frv = sb("frv", [P, Q])
        frstd = sb("frstd", [P, Q])
        out_sb = sb("out_sb", [P, Q, D])
        diag = sb("diag", [P, T], I32)
        a_sum = sb("a_sum", [P, G * PAIRS])
        a_junk = sb("a_junk", [P, CW], mybir.dt.bfloat16)
        ext = sb("ext", [P, 3])
        checks = sb("checks", [P, 5])
        held = sb("held", [P, 1])

        weights_loaded = sem("weights_loaded")
        biases_loaded = sem("biases_loaded")
        diag_loaded = sem("diag_loaded")
        x_loaded = [sem(f"x_loaded{i}") for i in range(G)]
        a_loaded = [sem(f"a_loaded{c}") for c in range(CHUNKS)]
        consts_ready = sem("consts_ready")
        vec_const = sem("vec_const")
        pe_const = sem("pe_const")
        norm_ready = sem("norm_ready")
        xt_ready = sem("xt_ready")
        xt_copied = sem("xt_copied")
        y0_ready = sem("y0_ready")
        sq_ready = sem("sq_ready")
        norm0 = sem("norm0")
        rstd_ready = sem("rstd_ready")
        y0_kept = sem("y0_kept")
        xhat_ready = sem("xhat_ready")
        exps_ready = sem("exps_ready")
        feat_ready = sem("feat_ready")
        diag_ready = sem("diag_ready")
        row_ready = sem("row_ready")
        r_ready = sem("r_ready")
        at_ready = sem("at_ready")
        e_ready = sem("e_ready")
        ev_ready = sem("ev_ready")
        p_ready = sem("p_ready")
        mm_done = sem("mm_done")
        a_checked = sem("a_checked")
        acc_copied = sem("acc_copied")
        fin_mm = sem("fin_mm")
        fin_step = sem("fin_step")
        stored = sem("stored")
        verdict = sem("verdict")
        verdict_pe = sem("verdict_pe")

        def quad_at(slot, first):
            i, odd = divmod(slot - first, 2)
            return i if not odd and 0 <= i < G else None

        with nc.Block() as block:

            @block.sync
            def _(sp):
                def load_x(i):
                    sp.dma_start(x_sb[:, Q * i:Q * (i + 1), :], x_t[:, Q * i:Q * (i + 1), :]).then_inc(x_loaded[i], 16)

                load_x(0)
                sp.dma_start(acol[:, 0:1], a1_col).then_inc(weights_loaded, 16)
                sp.dma_start(acol[:, 1:2], a2_col).then_inc(weights_loaded, 16)
                for dst, src in ((bcol[:, :], b_col), (brow[:, :], b_row), (ba[:, :], ba_11)):
                    sp.dma_start(dst, src).then_inc(biases_loaded, 16)

                def load(g, c):
                    sp.dma_start(a_sb[:, :, c * CW:(c + 1) * CW],
                                 adj[g * GW:(g + 1) * GW, c * CW:(c + 1) * CW]
                                 .rearrange("(q p) n -> p q n", p=P)).then_inc(a_loaded[c], 16)

                for i in range(1, X_FIRST):
                    load_x(i)
                load(0, 0)
                for i in range(X_FIRST, G):
                    load_x(i)
                for c in range(1, CHUNKS):
                    load(0, c)
                sp.dma_start(diag[:, :], diagonal, allow_slow_non_contiguous=True).then_inc(diag_loaded, 16)

                def store(g):
                    sp.wait_ge(fin_step, FIN * (g + 1))
                    sp.dma_start(out_t[:, g * Q:(g + 1) * Q, :], out_sb[:, :, :]).then_inc(stored, 16)

                for g in range(1, G):
                    for c in range(CHUNKS):
                        sp.wait_ge(at_ready, PAIRS * (g - 1) + PPC * (c + 1))
                        sp.wait_ge(a_checked, PAIRS * (g - 1) + PPC * (c + 1))
                        load(g, c)
                    if g >= 2:
                        store(g - 2)
                for g in (G - 2, G - 1):
                    store(g)
                sp.wait_ge(stored, 16 * G)

            @block.gpsimd
            def _(pool):
                nc.gpsimd.memset(ident[:, :], 0.0).then_inc(consts_ready, 1)
                nc.gpsimd.memset(last_row[:, :], 0.0).then_inc(consts_ready, 1)
                nc.gpsimd.memset(e_last[:, :], 0.0).then_inc(consts_ready, 1)
                nc.gpsimd.memset(ones[:, :], 1.0).then_inc(consts_ready, 1)
                nc.gpsimd.memset(minus1[:, :], -1.0).then_inc(consts_ready, 1)
                nc.gpsimd.memset(minus_half[:, :], -0.5).then_inc(consts_ready, 1)
                nc.gpsimd.memset(half[:, :], 0.5).then_inc(consts_ready, 1)
                pool.wait_ge(consts_ready, 7)
                nc.gpsimd.affine_select(out=ident[:, :], in_=ident[:, :], compare_op=ALU.not_equal, fill=1.0,
                                        base=0, pattern=[[-1, P]], channel_multiplier=1).then_inc(consts_ready, 1)
                nc.gpsimd.affine_select(out=last_row[:, :], in_=last_row[:, :], compare_op=ALU.not_equal, fill=-1.0,
                                        base=1 - P, pattern=[[0, P]], channel_multiplier=1).then_inc(consts_ready, 1)
                nc.gpsimd.memset(e_last[0:1, P - 1:P], 1.0).then_inc(consts_ready, 1)
                pool.wait_ge(vec_const, CS_READY)
                nc.gpsimd.tensor_tensor(norm_u[:, :], cs[:, 1:2], half[:, :], ALU.pow).then_inc(norm_ready, 1)

                def root(i):
                    pool.wait_ge(norm0, 2 * i + 2)
                    if i >= 2:
                        pool.wait_ge(xhat_ready, i - 1)
                    nc.gpsimd.tensor_tensor(rstd[:, i % 2, :], rv[:, i % 2, :],
                                            minus_half[:, :].broadcast_to([P, Q]), ALU.pow).then_inc(rstd_ready, 1)

                def features(i):
                    ts = slice(Q * i, Q * (i + 1))
                    pool.wait_ge(exps_ready, 2 * i + 1)
                    pool.wait_ge(xhat_ready, i + 1)
                    nc.gpsimd.tensor_tensor(feat[:, ts, 0:D - 1], xhat[:, ts, 0:D - 1],
                                            v_exp[:, ts].unsqueeze(2).broadcast_to([P, Q, D - 1]),
                                            ALU.mult).then_inc(feat_ready, 1)
                    nc.gpsimd.tensor_copy(feat[:, ts, D - 1], v_exp[:, ts]).then_inc(feat_ready, 1)

                for slot in range(FIRST_SLOT, PAIRS):
                    if (i := quad_at(slot, VARY)) is not None:
                        root(i)
                    if (i := quad_at(slot, FEATURES)) is not None:
                        features(i)
                with pool.Fori(0, G) as g:
                    pool.wait_ge(fin_step, FIN * g + FIN - 1)
                    nc.gpsimd.tensor_tensor(frstd[:, :], frv[:, :],
                                            minus_half[:, :].broadcast_to([P, Q]), ALU.pow).then_inc(rstd_ready, 1)

            @block.scalar
            def _(act):
                act.dma_start(w_nat[:, :], W).then_inc(weights_loaded, 16)
                act.dma_start(wv[:, :], Wv).then_inc(weights_loaded, 16)

                def copy_xt(i):
                    act.wait_ge(xt_ready, i + 1)
                    if i >= 2:
                        act.wait_ge(y0_ready, i - 1)
                    nc.scalar.copy(x_tr[:, i % 2, :], ps_xt[:, :]).then_inc(xt_copied, 1)

                def square(i):
                    act.wait_ge(y0_kept, i + 1)
                    if i >= 2:
                        act.wait_ge(norm0, 2 * (i - 2) + 1)
                    nc.scalar.activation(sq[:, i % 2, :].rearrange("p (q d) -> p q d", q=Q),
                                         xhat[:, Q * i:Q * (i + 1), :],
                                         ACT.Square).then_inc(sq_ready, 1)

                def column_exps(i):
                    act.wait_ge(xhat_ready, i + 1)
                    if i == 0:
                        act.wait_ge(vec_const, BIASES)
                    ts = slice(Q * i, Q * (i + 1))
                    nc.scalar.activation(v_exp[:, ts], st_cols[:, ts, 1], ACT.Exp, bias=bias[:, 1:2],
                                         scale=SLOPE).then_inc(exps_ready, 1)
                    nc.scalar.activation(w_exp[:, ts], st_cols[:, ts, 1], ACT.Exp, bias=bias[:, 0:1],
                                         scale=1 - SLOPE).then_inc(exps_ready, 1)

                def row_exps(g, src):
                    act.wait_ge(row_ready, g + 1)
                    nc.scalar.activation(R[:, :], src[:, :], ACT.Exp, bias=bias[:, 3:4],
                                         scale=1 - SLOPE).then_inc(r_ready, 1)

                def copy_acc(odd):
                    nc.scalar.copy(acc_t[:, :], ps_acc[odd][:, :]).then_inc(acc_copied, 1)

                def check_values(g, p, first):
                    c, q = divmod(p, PPC)
                    if q == 0:
                        act.wait_ge(a_loaded[c], 16 * (g + 1))
                    if not (first and p == 0):
                        act.wait_ge(a_checked, PAIRS * g + p)
                    nc.scalar.activation(a_junk[:, :], a_sb[:, q, c * CW:(c + 1) * CW], ACT.Square,
                                         bias=minus_half[:, :],
                                         accum_out=a_sum[:, bass.ds(g * PAIRS + p, 1)]).then_inc(a_checked, 1)

                def pair(g, p, odd, first=False):
                    if p == 0:
                        act.wait_ge(r_ready, g + 1)
                    if first and p % 2 == 0:
                        act.wait_ge(exps_ready, p + 2)
                    if p not in BY_VECTOR:
                        if not (first and p < NE):
                            act.wait_ge(mm_done, PAIRS * g + p - NE + 1)
                        for side in range(2):
                            ins = nc.scalar.activation(e_sb[:, p % NE, side * GW:(side + 1) * GW],
                                                       R[:, :], ACT.Relu, bias=minus1[:, :],
                                                       scale=w_exp[:, 2 * p + side:2 * p + side + 1])
                        ins.then_inc(e_ready, 1)
                    if p == COPY_AT and not first:
                        act.wait_ge(mm_done, PAIRS * g)
                        copy_acc(not odd)
                    check_values(g, p, first)

                def next_rows(g, src=ps_row):
                    act.wait_ge(e_ready, N_ACT * (g + 1))
                    act.wait_ge(ev_ready, N_VEC * (g + 1))
                    row_exps(g + 1, src)

                for slot in range(FIRST_SLOT, PAIRS):
                    if (i := quad_at(slot, COPY)) is not None:
                        copy_xt(i)
                    if (i := quad_at(slot, SQUARE)) is not None:
                        square(i)
                    if (i := quad_at(slot, EXPS)) is not None:
                        column_exps(i)
                    if slot == EXPS:
                        row_exps(0, ps_acc[0])
                    if slot >= 0:
                        pair(0, slot, odd=False, first=True)
                next_rows(0, ps_acc[1])
                with act.Fori(0, G // 2 - 1) as k:
                    for odd in (True, False):
                        g = 2 * k + 2 - odd
                        for p in range(PAIRS):
                            pair(g, p, odd)
                        next_rows(g)
                for p in range(PAIRS):
                    pair(G - 1, p, odd=True)
                act.wait_ge(mm_done, PAIRS * G)
                copy_acc(odd=True)

            @block.vector
            def _(dve):
                done = [0]

                def step(ins, s=vec_const):
                    done[0] += 1
                    ins.then_inc(s, 1)
                    dve.wait_ge(s, done[0])

                def centre(dst, src, c):
                    step(nc.vector.reduce_sum(mean[:, c:c + 1], src, AX))
                    step(nc.vector.tensor_scalar(mean[:, c + 1:c + 2], mean[:, c:c + 1], 1.0 / D, None, ALU.mult))
                    step(nc.vector.tensor_scalar(dst, src, mean[:, c + 1:c + 2], None, ALU.subtract))

                dve.wait_ge(consts_ready, 10)
                step(nc.vector.tensor_tensor(less_last[:, :], ident[:, :], last_row[:, :], ALU.add))
                dve.wait_ge(weights_loaded, 16 * 4)
                step(nc.vector.tensor_tensor(m0[:, :], wv[:, :], ident[:, :], ALU.add))
                centre(m0c, m0[:, :], 0)
                assert done[0] == M0_READY
                dve.wait_ge(pe_const, 1)
                step(nc.vector.tensor_copy(u[:, :], ps_misc[:, D:D + 2]))
                nc.vector.tensor_tensor(bb[:, 0:1], acol[:, 0:1], acol[:, 1:2], ALU.add).then_inc(vec_const, 1)
                done[0] += 1
                step(nc.vector.tensor_tensor(bb[:, 1:2], u[:, 1:2], u[:, 1:2], ALU.mult))
                dve.wait_ge(biases_loaded, 16 * 3)
                step(nc.vector.tensor_tensor(bb[:, 0:1], bb[:, 0:1], bcol[:, :], ALU.mult))
                assert done[0] == U_READY
                step(nc.vector.tensor_copy(w_t[:, :], ps_misc[:, 0:D]))
                dve.wait_ge(pe_const, 2)
                step(nc.vector.tensor_copy(m0c_t[:, :], ps_misc[:, 2 * D:3 * D]))
                assert done[0] == M0T_READY
                dve.wait_ge(pe_const, 3)
                step(nc.vector.tensor_copy(um, ps_misc[:, D:D + 2]))
                step(nc.vector.tensor_copy(cs[:, :], ps_misc[:, D + 2:D + 4]))
                assert done[0] == CS_READY

                def biases():
                    dve.wait_ge(norm_ready, 1)
                    nc.vector.tensor_scalar(bias[:, 0:1], norm_u[:, :], (SLOPE - 1) * D ** 0.5, None,
                                            ALU.mult).then_inc(vec_const, 1)
                    nc.vector.tensor_scalar(bias[:, 1:2], norm_u[:, :], -SLOPE * D ** 0.5, None,
                                            ALU.mult).then_inc(vec_const, 1)
                    done[0] += 2
                    step(nc.vector.scalar_tensor_tensor(out=bias[:, 2:3], in0=norm_u[:, :], scalar=D ** 0.5,
                                                        in1=cs[:, 0:1], op0=ALU.mult, op1=ALU.add))
                    step(nc.vector.tensor_scalar(bias[:, 3:4], bias[:, 2:3], 1 - SLOPE, None, ALU.mult))
                    assert done[0] == BIASES
                    nc.vector.tensor_copy(ident16[:, :], ident[:, :]).then_inc(vec_const, 1)
                    done[0] += 1

                def weights2():
                    dve.wait_ge(pe_const, 4)
                    step(nc.vector.tensor_copy(w2[:, :], ps_w2[:, 0:D]))
                    assert done[0] == W2_READ
                    centre(w2c, w2[:, :], 2)
                    step(nc.vector.tensor_copy(pick_den, ident[:, P - 1:P]))

                def keep(i):
                    dve.wait_ge(y0_ready, i + 1)
                    nc.vector.tensor_copy(xhat_st[:, Q * i:Q * (i + 1), :], ps_quad[:, :, 0:D + 2]).then_inc(y0_kept, 1)

                def variance(i):
                    k = i % 2
                    dve.wait_ge(sq_ready, i + 1)
                    if i >= 2:
                        dve.wait_ge(rstd_ready, i - 1)
                    nc.vector.reduce_sum(ss[:, k, :], sq[:, k, :].rearrange("p (q d) -> p q d", q=Q),
                                         AX).then_inc(norm0, 1)
                    dve.wait_ge(norm0, 2 * i + 1)
                    nc.vector.tensor_scalar(rv[:, k, :], ss[:, k, :], 1.0 / D, EPS, ALU.mult,
                                            ALU.add).then_inc(norm0, 1)

                def divide(i):
                    k = i % 2
                    ts = slice(Q * i, Q * (i + 1))
                    dve.wait_ge(rstd_ready, i + 1)
                    nc.vector.tensor_tensor(xhat_st[:, ts, :], xhat_st[:, ts, :],
                                            rstd[:, k, :].unsqueeze(2).broadcast_to([P, Q, D + 2]),
                                            ALU.mult).then_inc(xhat_ready, 1)

                def diagonals(g, first=False):
                    if first:
                        dve.wait_ge(xhat_ready, 1)
                    else:
                        dve.wait_ge(row_ready, g)
                    nc.vector.tensor_tensor(s_diag[:, :, :], ident[:, :].unsqueeze(1).broadcast_to([P, Q, P]),
                                            st_cols[:, bass.ds(g * Q, Q), 0:1].broadcast_to([P, Q, P]),
                                            ALU.mult).then_inc(diag_ready, 1)

                def finish(g, n, first=False):
                    if n == 0:
                        dve.wait_ge(fin_mm, g + 1)
                    else:
                        dve.wait_ge(fin_step, FIN * g + n)
                    if n == 0:
                        ins = nc.vector.tensor_scalar(den[:, :], ps_quad[:, :, D], FLT_MIN, None, ALU.max)
                    elif n == 1:
                        ins = nc.vector.reciprocal(rden[:, :], den[:, :])
                    elif n == 2:
                        ins = nc.vector.tensor_tensor(y[:, :, :], ps_quad[:, :, 0:D],
                                                      rden[:, :].unsqueeze(2).broadcast_to([P, Q, D]), ALU.mult)
                    elif n == 3:
                        ins = nc.vector.tensor_tensor(y[:, :, :], y[:, :, :], xhat[:, bass.ds(g * Q, Q), :], ALU.add)
                    elif n == 4:
                        ins = nc.vector.tensor_tensor(ysq[:, :, :], y[:, :, :], y[:, :, :], ALU.mult)
                    elif n == 5:
                        ins = nc.vector.reduce_sum(fss[:, :], ysq[:, :, :], AX)
                    elif n == 6:
                        ins = nc.vector.tensor_scalar(frv[:, :], fss[:, :], 1.0 / D, EPS, ALU.mult, ALU.add)
                    else:
                        dve.wait_ge(rstd_ready, G + g + 1)
                        if not first:
                            dve.wait_ge(stored, 16 * g)
                        ins = nc.vector.tensor_tensor(out_sb[:, :, :], y[:, :, :],
                                                      frstd[:, :].unsqueeze(2).broadcast_to([P, Q, D]), ALU.mult)
                    ins.then_inc(fin_step, 1)

                def pair(g, p, first=False):
                    e = e_sb[:, p % NE, :]
                    if p in BY_VECTOR:
                        n = BY_VECTOR.index(p)
                        dve.wait_ge(r_ready, g + 1)
                        if first:
                            dve.wait_ge(exps_ready, 2 * (p // 2) + 2)
                        if not (first and p < NE):
                            dve.wait_ge(mm_done, PAIRS * g + p - NE + 1)
                        for side in range(2):
                            ins = nc.vector.tensor_scalar(e[:, side * GW:(side + 1) * GW], R[:, :],
                                                          w_exp[:, 2 * p + side:2 * p + side + 1], 1.0, ALU.mult,
                                                          ALU.max)
                        ins.then_inc(ev_ready, 1)
                        dve.wait_ge(ev_ready, N_VEC * g + n + 1)
                        plus = 0.0
                    else:
                        dve.wait_ge(e_ready, N_ACT * g + BY_SCALAR.index(p) + 1)
                        plus = 1.0
                    dve.wait_ge(at_ready, PAIRS * g + p + 1)
                    nc.vector.scalar_tensor_tensor(out=e, in0=e, scalar=plus, in1=ps_at_int[p % NA],
                                                   op0=ALU.add, op1=ALU.mult).then_inc(p_ready, 1)

                def group(g, second=False, last=False):
                    for p in range(PAIRS):
                        pair(g, p)
                        if FIN_AT <= p < FIN_AT + FIN - 1:
                            finish(g - 1, p - FIN_AT, first=second)
                        if p == FIN_AT + FIN:
                            finish(g - 1, FIN - 1, first=second)
                        if p == DIAG_AT and not last:
                            diagonals(g + 1)

                for slot in range(FIRST_SLOT, PAIRS):
                    if (i := quad_at(slot, KEEP)) is not None:
                        keep(i)
                    if slot == KEEP:
                        weights2()
                    if (i := quad_at(slot, VARY)) is not None:
                        variance(i)
                    if slot == VARY:
                        biases()
                    if (i := quad_at(slot, DIVIDE)) is not None:
                        divide(i)
                    if slot == DIVIDE:
                        diagonals(0, first=True)
                    if slot >= 0:
                        pair(0, slot, first=True)
                    if slot == DIAG_AT:
                        diagonals(1)
                group(1, second=True)
                with dve.Fori(2, G - 1) as g:
                    group(g)
                group(G - 1, last=True)

                done[0] = 0
                dve.wait_ge(a_checked, G * PAIRS)
                dve.wait_ge(diag_loaded, 16)
                nc.vector.tensor_reduce(ext[:, 0:1], st_cols[:, :, 1], AX, ALU.min).then_inc(verdict, 1)
                nc.vector.tensor_reduce(ext[:, 1:2], st_cols[:, :, 0], AX, ALU.max).then_inc(verdict, 1)
                nc.vector.tensor_reduce(ext[:, 2:3], st_cols[:, :, 0], AX, ALU.min).then_inc(verdict, 1)
                nc.vector.reduce_max(checks[:, 0:1], a_sum[:, :], AX).then_inc(verdict, 1)
                nc.vector.tensor_reduce(checks[:, 1:2], diag[:, :], AX, ALU.min).then_inc(verdict, 1)
                done[0] += 5
                dve.wait_ge(verdict, done[0])
                nc.vector.scalar_tensor_tensor(out=checks[:, 2:3], in0=norm_u[:, :], scalar=D ** 0.5, in1=ext[:, 0:1],
                                               op0=ALU.mult, op1=ALU.subtract).then_inc(verdict, 1)
                nc.vector.tensor_tensor(checks[:, 3:4], ext[:, 1:2], bias[:, 2:3], ALU.add).then_inc(verdict, 1)
                nc.vector.scalar_tensor_tensor(out=checks[:, 4:5], in0=ext[:, 2:3], scalar=-1.0, in1=bias[:, 2:3],
                                               op0=ALU.mult, op1=ALU.subtract).then_inc(verdict, 1)
                done[0] += 3
                dve.wait_ge(verdict, done[0])
                nc.vector.tensor_scalar(checks[:, 0:1], checks[:, 0:1], CW / 4.0, None,
                                        ALU.is_le).then_inc(verdict, 1)
                nc.vector.tensor_scalar(checks[:, 1:2], checks[:, 1:2], 1.0, None, ALU.is_ge).then_inc(verdict, 1)
                nc.vector.tensor_scalar(checks[:, 2:5], checks[:, 2:5], LIMIT, None, ALU.is_le).then_inc(verdict, 1)
                done[0] += 3
                dve.wait_ge(verdict, done[0])
                step(nc.vector.reduce_sum(held[:, :], checks[:, :], AX), verdict)
                assert done[0] == CHECKS_READY
                for n in range(FIN):
                    finish(G - 1, n)
                dve.wait_ge(verdict_pe, 1)
                total = float(5 * P)
                if force_general:
                    total += 1.0
                step(nc.vector.tensor_scalar(flag[:, :], ps_acc[0][0:1, 0:1], total, None, ALU.not_equal), verdict)

            @block.tensor
            def _(pe):
                pe.wait_ge(consts_ready, 10)

                def x_transposed(i):
                    pe.wait_ge(x_loaded[i], 16)
                    if i >= 1:
                        pe.wait_ge(xt_copied, i)
                    for q in range(Q):
                        ins = nc.tensor.transpose(ps_xt[:, q * P:(q + 1) * P], x_sb[:, Q * i + q, :], ident[:, :])
                    ins.then_inc(xt_ready, 1)

                def layer0(i):
                    pe.wait_ge(xt_copied, i + 1)
                    if i == 0:
                        pe.wait_ge(vec_const, CS_READY)
                    else:
                        pe.wait_ge(y0_kept, i)
                    for q in range(Q):
                        ins = nc.tensor.matmul(ps_quad[:, q, 0:D + 2],
                                               x_tr[:, i % 2, q * P:(q + 1) * P], m0c_um[:, :], start=True, stop=True)
                    ins.then_inc(y0_ready, 1)

                def spread(g, dst=ps_row, first=False, second=False):
                    pe.wait_ge(diag_ready, g + 1)
                    if first:
                        pe.wait_ge(vec_const, W2_READ)
                    elif second:
                        pe.wait_ge(xt_copied, G)
                    else:
                        pe.wait_ge(fin_step, FIN * (g - 2) + 3)
                    nc.tensor.matmul(dst[:, :], ones[:, :], s_diag[:, :, :].rearrange("p q n -> p (q n)"),
                                     start=True, stop=True).then_inc(row_ready, 1)

                def weights():
                    pe.wait_ge(weights_loaded, 16 * 4)
                    nc.tensor.transpose(ps_misc[:, 0:D], w_nat[:, :], ident[:, :])
                    nc.tensor.matmul(ps_misc[:, D:D + 2], w_nat[:, :], acol[:, :], start=True,
                                     stop=True).then_inc(pe_const, 1)
                    pe.wait_ge(vec_const, U_READY + 1)
                    nc.tensor.transpose(ps_misc[:, 2 * D:3 * D], m0c, ident[:, :]).then_inc(pe_const, 1)
                    pe.wait_ge(vec_const, M0T_READY)
                    nc.tensor.matmul(ps_misc[:, D:D + 2], m0c_t[:, :], u[:, :], start=True, stop=True)
                    nc.tensor.matmul(ps_misc[:, D + 2:D + 4], ones[:, :], bb[:, :], start=True, stop=False,
                                     skip_group_check=True)
                    nc.tensor.matmul(ps_misc[:, D + 2:D + 3], ones[0:1, :], ba[:, :], start=False, stop=True,
                                     skip_group_check=True).then_inc(pe_const, 1)
                    nc.tensor.matmul(ps_w2[:, 0:D], less_last[:, :], w_t[:, :], start=True, stop=False)
                    nc.tensor.matmul(ps_w2[:, 0:D], e_last[:, :], brow[:, :], start=False,
                                     stop=True).then_inc(pe_const, 1)

                half_words = a_sb[:, :, :].rearrange("p q n -> p (q n)").bitcast(F16).rearrange(
                    "p (q n two) -> p q n two", q=Q, two=2)[:, :, :, 0]

                def pair(g, p, first=False):
                    if p % PPC == 0:
                        pe.wait_ge(a_loaded[p // PPC], 16 * (g + 1))
                    if first and p == 0:
                        pe.wait_ge(vec_const, BIASES + 1)
                    for side in range(2):
                        for q in range(Q):
                            j = (2 * p + side) * P
                            c = side * GW + q * P
                            ins = nc.tensor.transpose(ps_at[p % NA][:, c:c + P], half_words[:, q, j:j + P],
                                                      ident16[:, :])
                    ins.then_inc(at_ready, 1)

                def sums(g, p, odd, first=False, second=False):
                    if p == 0:
                        if first:
                            pe.wait_ge(r_ready, 1)
                        elif second:
                            pe.wait_ge(r_ready, 2)
                        else:
                            pe.wait_ge(acc_copied, g - 1)
                    if first and p % 2 == 0:
                        pe.wait_ge(feat_ready, 2 * (p // 2 + 1))
                    pe.wait_ge(p_ready, PAIRS * g + p + 1)
                    for side in range(2):
                        j = 2 * p + side
                        ins = nc.tensor.matmul(ps_acc[odd][:, :], feat[:, j, :], e_sb[:, p % NE, side * GW:(side + 1) * GW],
                                               start=(j == 0), stop=(j == T - 1))
                    ins.then_inc(mm_done, 1)

                def project(g, first=False, last=False):
                    pe.wait_ge(acc_copied, g + 1)
                    if first:
                        pe.wait_ge(xhat_ready, G)
                    if last:
                        pe.wait_ge(fin_step, FIN * (g - 1) + 3)
                    else:
                        pe.wait_ge(r_ready, g + 2)
                    for q in range(Q):
                        ins = nc.tensor.matmul(ps_quad[:, q, 0:D + 1], acc_t[:, q * P:(q + 1) * P], w2c_den[:, :],
                                               start=True, stop=True)
                    ins.then_inc(fin_mm, 1)

                def group(g, odd, second=False, last=False):
                    for p in range(PAIRS):
                        n = p + AHEAD
                        if n < PAIRS:
                            pair(g, n)
                        elif not last:
                            pair(g + 1, n - PAIRS)
                        sums(g, p, odd, second=second)
                        if p == PROJECT_AT:
                            project(g - 1, first=second)
                        if p == SPREAD_AT and not last:
                            spread(g + 1)

                for slot in range(FIRST_SLOT, PAIRS):
                    if (i := quad_at(slot, TURN)) is not None:
                        x_transposed(i)
                    if slot == FIRST_SLOT:
                        weights()
                    if (i := quad_at(slot, MULTIPLY)) is not None:
                        layer0(i)
                    if slot == SPREAD0_AT:
                        spread(0, dst=ps_acc[0], first=True)
                    n = slot + AHEAD
                    if n >= PAIRS:
                        pair(1, n - PAIRS)
                    elif n >= 0:
                        pair(0, n, first=True)
                    if slot >= 0:
                        sums(0, slot, odd=False, first=True)
                    if slot == SPREAD_AT:
                        spread(1, dst=ps_acc[1], second=True)
                group(1, odd=True, second=True)
                group(2, odd=False)
                with pe.Fori(1, G // 2 - 1) as k:
                    for odd in (True, False):
                        group(2 * k + 2 - odd, odd)
                group(G - 1, odd=True, last=True)
                project(G - 1, last=True)
                pe.wait_ge(verdict, CHECKS_READY)
                nc.tensor.matmul(ps_acc[0][0:1, 0:1], held[:, :], ones[:, 0:1], start=True,
                                 stop=True).then_inc(verdict_pe, 1)

        xhat_t = sb("xhat_t", [P, N])
        wq = sb("wq", [P, D])
        wk = sb("wk", [P, D])
        q_cur = sb("q_cur", [P, P])
        u2_rep = sb("u2_rep", [P, P])
        s_cur = sb("s_cur", [P, 1])
        s_col = sb("s_col", [P, T])
        neg_max = sb("neg_max", [P, 1])
        row_sum = sb("row_sum", [P, 1])
        a_row = a_sb[:, 0, :]
        scores_row = a_sb[:, 1, :].bitcast(F32)
        k_t = a_sb[:, 2, :].bitcast(F32)
        q_t = a_sb[:, 3, :].bitcast(F32)
        pairs_flat = e_sb[:, :, :].rearrange("p n c -> p (n c)")
        p_t = pairs_flat[:, 0:N]
        mask = pairs_flat[:, N:2 * N]
        values = feat
        yg, yg2 = y[:, 0, :], y[:, 1, :]

        g_loaded = sem("g_loaded")
        g_made = sem("g_made")
        g_kept = sem("g_kept")
        g_small = sem("g_small")
        g_adj = [sem(f"g_adj{n}") for n in range(2)]
        g_query = [sem(f"g_query{n}") for n in range(2)]
        g_prod = [sem(f"g_prod{n}") for n in range(2)]
        g_vec = [sem(f"g_vec{n}") for n in range(2)]
        g_exp = [sem(f"g_exp{n}") for n in range(2)]
        g_pt = [sem(f"g_pt{n}") for n in range(2)]
        g_pt_kept = [sem(f"g_pt_kept{n}") for n in range(2)]
        g_sums = [sem(f"g_sums{n}") for n in range(2)]
        g_rstd = [sem(f"g_rstd{n}") for n in range(2)]
        g_stored = sem("g_stored")
        KEPT = [4 * G, 7 * G]
        SCORED = [16, 10]
        VARIED = [25, 19]
        ROWS = [26, 20]

        def if_general(eng):
            return eng.If(eng.value_load(flag[0:1, 0:1]) != 0)

        with nc.Block() as block:

            @block.tensor
            def _(pe):
                with if_general(pe):
                    made = [0]

                    def product(ins):
                        made[0] += 1
                        ins.then_inc(g_made, 1)
                        pe.wait_ge(g_kept, made[0])

                    def turned(src):
                        for i in range(G):
                            for q in range(Q):
                                ins = nc.tensor.transpose(bank[0][:, q * P:(q + 1) * P], src[:, Q * i + q, :],
                                                          ident[:, :])
                            product(ins)

                    def by_rows(w):
                        for i in range(G):
                            product(nc.tensor.matmul(bank[0][:, :], w[:, :], xhat_t[:, i * GW:(i + 1) * GW],
                                                     start=True, stop=True))

                    def by_cols(w, bias_row):
                        for i in range(G):
                            for q in range(Q):
                                t = Q * i + q
                                dst = bank[0][:, q * P:(q + 1) * P]
                                ins = nc.tensor.matmul(dst, xhat_t[:, t * P:(t + 1) * P], w[:, :], start=True,
                                                       stop=bias_row is None)
                                if bias_row is not None:
                                    ins = nc.tensor.matmul(dst, ones[0:1, :], bias_row[:, :], start=False, stop=True)
                            product(ins)

                    def tiles(n):
                        with pe.Fori(0, T) as t:
                            if n == 0:
                                pe.wait_ge(g_query[n], t + 1)
                                for c in range(G):
                                    nc.tensor.matmul(bank[c][:, :], q_cur[:, :], k_t[:, c * GW:(c + 1) * GW],
                                                     start=True, stop=True).then_inc(g_prod[n], 1)
                            pe.wait_ge(g_exp[n], t + 1)
                            for c in range(G):
                                for q in range(Q):
                                    j = Q * c + q
                                    ins = nc.tensor.transpose(bank[c][:, q * P:(q + 1) * P],
                                                              scores_row[:, j * P:(j + 1) * P], ident[:, :])
                                ins.then_inc(g_pt[n], 1)
                            pe.wait_ge(g_pt_kept[n], G * (t + 1))
                            for j in range(T):
                                ins = nc.tensor.matmul(bank[0][:, 0:D], p_t[:, j * P:(j + 1) * P], values[:, j, :],
                                                       start=(j == 0), stop=(j == T - 1))
                            ins.then_inc(g_sums[n], 1)
                            pe.wait_ge(g_vec[n], ROWS[n] * (t + 1))

                    pe.wait_ge(g_loaded, 32)
                    turned(x_sb)
                    by_rows(wq)
                    by_rows(wk)
                    by_cols(wv, None)
                    tiles(0)
                    turned(xhat)
                    pe.wait_ge(g_small, 1)
                    by_rows(u2_rep)
                    by_cols(w_t, brow)
                    assert made[0] == KEPT[1]
                    for t in range(T):
                        ins = nc.tensor.matmul(bank[1][:, t:t + 1], xhat_t[:, t * P:(t + 1) * P], u[:, 0:1],
                                               start=True, stop=True)
                    ins.then_inc(g_made, 1)
                    tiles(1)

            @block.scalar
            def _(act):
                with if_general(act):
                    kept = [0]

                    def keep(dst):
                        kept[0] += 1
                        act.wait_ge(g_made, kept[0])
                        nc.scalar.copy(dst, bank[0][:, :]).then_inc(g_kept, 1)

                    def keep_all(dst):
                        for i in range(G):
                            keep(dst(i))

                    def cols(buf):
                        return lambda i: buf[:, i * GW:(i + 1) * GW]

                    def by_tile(buf):
                        return lambda i: buf[:, Q * i:Q * (i + 1), :].rearrange("p q d -> p (q d)")

                    def tiles(n):
                        with act.Fori(0, T) as t:
                            act.dma_start(a_row, adj[bass.ds(t * P, P), :]).then_inc(g_adj[n], 16)
                            act.wait_ge(g_vec[n], ROWS[n] * t + SCORED[n])
                            nc.scalar.activation(scores_row, scores_row, ACT.Exp,
                                                 accum_out=row_sum[:, :]).then_inc(g_exp[n], 1)
                            for c in range(G):
                                act.wait_ge(g_pt[n], G * t + c + 1)
                                nc.scalar.copy(p_t[:, c * GW:(c + 1) * GW], bank[c][:, :]).then_inc(g_pt_kept[n], 1)
                            act.wait_ge(g_vec[n], ROWS[n] * (t + 1))
                            if n == 1:
                                act.dma_start(out_t[:, bass.ds(t, 1), :], out_sb[:, 0:1, :]).then_inc(g_stored, 16)
                                act.wait_ge(g_stored, 16 * (t + 1))

                    keep_all(cols(xhat_t))
                    keep_all(cols(q_t))
                    keep_all(cols(k_t))
                    keep_all(by_tile(values))
                    assert kept[0] == KEPT[0]
                    tiles(0)
                    keep_all(cols(xhat_t))
                    keep_all(cols(k_t))
                    keep_all(by_tile(values))
                    tiles(1)

            @block.sync
            def _(sp):
                with if_general(sp):
                    sp.dma_start(wq[:, :], Wq).then_inc(g_loaded, 16)
                    sp.dma_start(wk[:, :], Wk).then_inc(g_loaded, 16)
                    sp.wait_ge(g_loaded, 32)

            @block.gpsimd
            def _(pool):
                with if_general(pool):
                    for n in range(2):
                        with pool.Fori(0, T) as t:
                            pool.wait_ge(g_vec[n], ROWS[n] * t + VARIED[n])
                            nc.gpsimd.tensor_tensor(frstd[:, 0:1], frv[:, 0:1], minus_half[:, :],
                                                    ALU.pow).then_inc(g_rstd[n], 1)

            @block.vector
            def _(dve):
                with if_general(dve):
                    def tiles(n):
                        dve.wait_ge(g_kept, KEPT[n])
                        with dve.Fori(0, T) as t:
                            done = [0]

                            def step(ins):
                                done[0] += 1
                                ins.then_inc(g_vec[n], 1)
                                dve.wait_ge(g_vec[n], ROWS[n] * t + done[0])

                            if n == 0:
                                step(nc.vector.tensor_copy(q_cur[:, :], q_t[:, bass.ds(t * P, P)]))
                                dve.sem_inc(g_query[n], 1)
                                dve.wait_ge(g_adj[n], 16 * (t + 1))
                                step(nc.vector.tensor_copy(mask, a_row))
                                own = pairs_flat[:, bass.ds(t * P + N, P)]
                                step(nc.vector.tensor_tensor(own, own, ident[:, :], ALU.add))
                                step(nc.vector.tensor_scalar(mask, mask, -1.0, -1.0, ALU.add, ALU.max))
                                step(nc.vector.tensor_scalar(mask, mask, 1.0, FLT_MAX, ALU.min, ALU.mult))
                                for c in range(G):
                                    dve.wait_ge(g_prod[n], G * t + c + 1)
                                    cc = slice(c * GW, (c + 1) * GW)
                                    step(nc.vector.tensor_tensor(scores_row[:, cc], bank[c][:, :], mask[:, cc],
                                                                 ALU.add))
                            else:
                                step(nc.vector.tensor_copy(s_cur[:, :], s_col[:, bass.ds(t, 1)]))
                                step(nc.vector.tensor_scalar(scores_row, k_t, s_cur[:, :], None, ALU.add))
                                step(nc.vector.scalar_tensor_tensor(out=scores_row, in0=scores_row, scalar=SLOPE,
                                                                    in1=scores_row, op0=ALU.mult, op1=ALU.max))
                                dve.wait_ge(g_adj[n], 16 * (t + 1))
                                step(nc.vector.tensor_scalar(mask, a_row, 0.0, None, ALU.is_gt))
                                step(nc.vector.tensor_tensor(scores_row, scores_row, mask, ALU.mult))
                                step(nc.vector.tensor_scalar(mask, mask, -1.0, NEG, ALU.add, ALU.mult))
                                step(nc.vector.tensor_tensor(scores_row, scores_row, mask, ALU.add))
                            step(nc.vector.reduce_max(neg_max[:, :], scores_row, AX))
                            step(nc.vector.tensor_scalar(neg_max[:, :], neg_max[:, :], -1.0, None, ALU.mult))
                            step(nc.vector.tensor_scalar(scores_row, scores_row, neg_max[:, :], -FLT_MAX, ALU.add,
                                                         ALU.max))
                            assert done[0] == SCORED[n]
                            dve.wait_ge(g_sums[n], t + 1)
                            step(nc.vector.reciprocal(rden[:, 0:1], row_sum[:, :]))
                            step(nc.vector.tensor_scalar(yg, bank[0][:, 0:D], rden[:, 0:1], None, ALU.mult))
                            x_in = x_sb if n == 0 else xhat
                            step(nc.vector.tensor_tensor(y[:, 0:1, :], y[:, 0:1, :], x_in[:, bass.ds(t, 1), :],
                                                         ALU.add))
                            step(nc.vector.reduce_sum(mean[:, 0:1], yg, AX))
                            step(nc.vector.tensor_scalar(mean[:, 1:2], mean[:, 0:1], 1.0 / D, None, ALU.mult))
                            step(nc.vector.tensor_scalar(yg, yg, mean[:, 1:2], None, ALU.subtract))
                            step(nc.vector.tensor_tensor(yg2, yg, yg, ALU.mult))
                            step(nc.vector.reduce_sum(fss[:, 0:1], yg2, AX))
                            step(nc.vector.tensor_scalar(frv[:, 0:1], fss[:, 0:1], 1.0 / D, EPS, ALU.mult, ALU.add))
                            assert done[0] == VARIED[n]
                            dve.wait_ge(g_rstd[n], t + 1)
                            dst = xhat[:, bass.ds(t, 1), :] if n == 0 else out_sb[:, 0:1, :]
                            step(nc.vector.tensor_scalar(dst, y[:, 0:1, :], frstd[:, 0:1], None, ALU.mult))
                            assert done[0] == ROWS[n]

                    tiles(0)
                    nc.vector.tensor_scalar(u2_rep[:, :], ones[:, :], u[:, 1:2], None, ALU.mult).then_inc(g_small, 1)
                    dve.wait_ge(g_kept, KEPT[1])
                    dve.wait_ge(g_made, KEPT[1] + 1)
                    nc.vector.tensor_scalar(s_col[:, :], bank[1][:, 0:T], cs[:, 0:1], None,
                                            ALU.add).then_inc(g_small, 1)
                    dve.wait_ge(g_small, 2)
                    tiles(1)


_INS = ['x', 'adj', 'L0_gnn_Wq', 'L0_gnn_Wk', 'L0_gnn_Wv', 'L1_gnn_W', 'L1_gnn_b_W', 'L1_gnn_a_vec', 'L1_gnn_b_a']


def kernel(**inputs):
    import numpy as _np
    import concourse.bacc as _bacc
    from concourse import mybir as _mybir
    from concourse.bass_utils import run_bass_kernel_spmd as _run

    nc = _bacc.Bacc("TRN2", target_bir_lowering=False, num_devices=1)
    arrays, args = {}, []
    for name in _INS:
        a = _np.ascontiguousarray(inputs[name])
        arrays[f"in_{name}_dram"] = a
        args.append(nc.dram_tensor(f"in_{name}_dram", a.shape, _mybir.dt.from_np(a.dtype), kind="ExternalInput").ap())
    out = nc.dram_tensor("out_0_dram", inputs["x"].shape, _mybir.dt.float32, kind="ExternalOutput").ap()
    graph_layers(nc, args[0], args[1], args[2], args[3], args[4], args[5], args[6], args[7], args[8], out)
    r = _run(nc, [arrays], core_ids=[0])
    return r.results[0]["out_0_dram"]
```

```python
from contextlib import ExitStack

import numpy as np
import concourse.bass as bass
from concourse import mybir

F32 = mybir.dt.float32
F16 = mybir.dt.float16
I32 = mybir.dt.int32
I16 = mybir.dt.int16
ALU = mybir.AluOpType
ACT = mybir.ActivationFunctionType
AX = mybir.AxisListType.X

P = 128
EPS = 1e-5
SLOPE = 0.2
MAX_S = 13.5
MIN_S = -60.0
MAX_BELOW = 40.0
V_SCALE = 4096.0
FLT_MIN = float(np.finfo(np.float32).tiny)
FLT_MAX = float(np.finfo(np.float32).max)
NEG = 9e15


def graph_layers(nc, x, adj, Wq, Wk, Wv, W, b, a_vec, b_a, out, force_general=False):
    N, D = x.shape
    assert D == P and N % 512 == 0
    T = N // P
    Q = 4
    GW = Q * P
    G = N // GW
    PAIRS = T // 2
    CHUNKS = 4
    CW = N // CHUNKS
    PPC = PAIRS // CHUNKS
    NA = 4
    NE = 8
    AHEAD = NA
    SPLIT = list(range(1, PAIRS, 2))
    N_SPLIT = len(SPLIT)
    PARTS = 2
    CHECK_AT = 1
    NH = 4
    assert PAIRS % NA == 0 and PAIRS % NE == 0 and N_SPLIT % NH == 0 and PPC == Q
    assert 2 * NH == NE and Q == 4
    FIN = 8
    BY_VECTOR0 = [0, 2, 4, 6, 8, 10, 12, 14]
    BY_VECTOR = [0, 2, 4, 6, 8]

    def by_vector(g, p, first):
        if first:
            return sum(n <= p for n in BY_VECTOR0)
        return len(BY_VECTOR) * g + sum(n <= p for n in BY_VECTOR) + len(BY_VECTOR0) - len(BY_VECTOR)

    def by_scalar(g, p, first):
        if first:
            return p + 1 - by_vector(g, p, first)
        others = [n for n in range(PAIRS) if n not in BY_VECTOR]
        return len(others) * g + sum(n <= p for n in others) + len(BY_VECTOR) - len(BY_VECTOR0)

    COPY_AT, PROJECT_AT, FIN_AT = 6, 3, 7
    DIAG_AT, SPREAD_AT, R_AT = 2, 1, 7
    ROOT_AT = 11
    DIAG1_AT, SPREAD1_AT, R1_AT = 5, 8, 11
    FIRST_SLOT = TURN = -11
    COPY = -10
    MULTIPLY = -8
    KEEP = -6
    SQUARE = -6
    VARY = -5
    DIVIDE = -4
    SPREAD0_AT = -3
    EXPS = FEATURES = -2
    SPLIT_FEATURES = 1
    X_FIRST = 5
    M0_READY, U_READY, M0T_READY, CS_READY = 5, 9, 11, 13
    W2_READ, BIASES = 14, 23
    CHECKS_READY = 14

    x_t = x.rearrange("(t p) d -> p t d", p=P)
    out_t = out.rearrange("(t p) d -> p t d", p=P)
    a1_col = a_vec[0:D].rearrange("(p c) -> p c", c=1)
    a2_col = a_vec[D:2 * D].rearrange("(p c) -> p c", c=1)
    b_col = b.rearrange("(p c) -> p c", c=1)
    b_row = b.rearrange("(a d) -> a d", a=1)
    diagonal = adj.rearrange("i j -> (i j)")[0:N * N:N + 1].rearrange("(t p) -> p t", p=P)
    ba_11 = b_a.rearrange("(a d) -> a d", a=1)

    with ExitStack() as ctx:
        def sb(name, shape, dt=F32):
            return ctx.enter_context(nc.sbuf_tensor(name, shape, dt))

        def sem(name):
            return ctx.enter_context(nc.semaphore(name))

        banks = ctx.enter_context(nc.psum_tensor("banks", [P, 8, 512], F32))
        bank = [banks[:, i, :] for i in range(8)]
        ps_at = [bank[i][:, :].bitcast(F16) for i in range(NA)]
        ps_at_int = [bank[i][:, :].bitcast(I16) for i in range(NA)]
        ps_w2 = bank[4]
        ps_acc = [bank[4], bank[5]]
        ps_xt = bank[5]
        ps_quad = banks[:, 6:8, :].rearrange("p b (h c) -> p (b h) c", h=2)
        ps_row = bank[6]
        ps_misc = bank[7]

        ident = sb("ident", [P, P])
        ones = sb("ones", [P, P])
        wv = sb("wv", [P, D])
        w_nat = sb("w_nat", [P, D])
        w_t = sb("w_t", [P, D])
        acol = sb("acol", [P, 2])
        bcol = sb("bcol", [P, 1])
        brow = sb("brow", [1, D])
        ba = sb("ba", [1, 1])
        u = sb("u", [P, 2])
        bb = sb("bb", [P, 2])
        cs = sb("cs", [P, 2])
        flag = sb("flag", [1, 1], I32)
        a_sb = sb("a_sb", [P, Q, N], I32)
        x_sb = sb("x_sb", [P, T, D])
        xhat_st = sb("xhat_st", [P, T, D + 2])
        xhat, st_cols = xhat_st[:, :, 0:D], xhat_st[:, :, D:D + 2]
        feat = sb("feat", [P, T, D])
        R = sb("R", [P, 2, GW])
        e_sb = sb("e_sb", [P, NE, 2 * GW])
        p_parts = sb("p_parts", [P, 2, NH, 2 * GW], F16)
        ph, pl = p_parts[:, 0, :, :], p_parts[:, 1, :, :]
        fh = sb("fh", [P, T // 2, D], F16)
        fl = sb("fl", [P, T // 2, D], F16)
        x_tr = sb("x_tr", [P, 2, GW])
        sq = sb("sq", [P, 2, GW])
        last_row = sb("last_row", [P, P])
        less_last = sb("less_last", [P, P])
        e_last = sb("e_last", [1, P])
        ident16 = sb("ident16", [P, P], F16)
        m0 = sb("m0", [P, D])
        m0c_um = sb("m0c_um", [P, D + 2])
        m0c = m0c_um[:, 0:D]
        um = m0c_um[:, D:D + 2]
        m0c_t = sb("m0c_t", [P, D])
        w2 = sb("w2", [P, D])
        w2c_den = sb("w2c_den", [P, D + 1])
        w2c = w2c_den[:, 0:D]
        pick_den = w2c_den[:, D:D + 1]
        mean = sb("mean", [P, 4])
        ss = sb("ss", [P, 2, Q])
        rv = sb("rv", [P, 2, Q])
        rstd = sb("rstd", [P, 2, Q])
        s_diag = sb("s_diag", [P, Q, P])
        norm_u = sb("norm_u", [P, 1])
        bias = sb("bias", [P, 5])
        minus1 = sb("minus1", [P, 1])
        minus_half = sb("minus_half", [P, 1])
        half = sb("half", [P, 1])
        w_exp = sb("w_exp", [P, T])
        v_exp = sb("v_exp", [P, T])
        acc_t = sb("acc_t", [P, GW])
        y = sb("y", [P, Q, D])
        ysq = sb("ysq", [P, Q, D])
        den = sb("den", [P, Q])
        rden = sb("rden", [P, Q])
        fss = sb("fss", [P, Q])
        frv = sb("frv", [P, Q])
        frstd = sb("frstd", [P, Q])
        out_sb = sb("out_sb", [P, Q, D])
        diag = sb("diag", [P, T], I32)
        a_sum = sb("a_sum", [P, G * CHUNKS * PARTS])
        a_junk = sb("a_junk", [P, Q // PARTS, CW], mybir.dt.bfloat16)
        ext = sb("ext", [P, 3])
        checks = sb("checks", [P, 5])
        held = sb("held", [P, 1])

        weights_loaded = sem("weights_loaded")
        biases_loaded = sem("biases_loaded")
        diag_loaded = sem("diag_loaded")
        x_loaded = [sem(f"x_loaded{i}") for i in range(G)]
        a_loaded = [sem(f"a_loaded{c}") for c in range(CHUNKS)]
        consts_ready = sem("consts_ready")
        vec_const = sem("vec_const")
        pe_const = sem("pe_const")
        norm_ready = sem("norm_ready")
        xt_ready = sem("xt_ready")
        xt_copied = sem("xt_copied")
        y0_ready = sem("y0_ready")
        sq_ready = sem("sq_ready")
        norm0 = sem("norm0")
        rstd_ready = sem("rstd_ready")
        y0_kept = sem("y0_kept")
        xhat_ready = sem("xhat_ready")
        exps_ready = sem("exps_ready")
        feat_ready = sem("feat_ready")
        parts_ready = sem("parts_ready")
        diag_ready = sem("diag_ready")
        row_ready = sem("row_ready")
        r_ready = sem("r_ready")
        at_ready = sem("at_ready")
        e_ready = sem("e_ready")
        ev_ready = sem("ev_ready")
        p_ready = sem("p_ready")
        ph_ready = sem("ph_ready")
        pl_ready = sem("pl_ready")
        mm_done = sem("mm_done")
        a_checked = sem("a_checked")
        acc_copied = sem("acc_copied")
        fin_mm = sem("fin_mm")
        fin_step = sem("fin_step")
        stored = sem("stored")
        verdict = sem("verdict")
        verdict_pe = sem("verdict_pe")

        def quad_at(slot, first):
            i, odd = divmod(slot - first, 2)
            return i if not odd and 0 <= i < G else None

        with nc.Block() as block:

            @block.sync
            def _(sp):
                def load_x(i):
                    sp.dma_start(x_sb[:, Q * i:Q * (i + 1), :], x_t[:, Q * i:Q * (i + 1), :]).then_inc(x_loaded[i], 16)

                load_x(0)
                sp.dma_start(acol[:, 0:1], a1_col).then_inc(weights_loaded, 16)
                sp.dma_start(acol[:, 1:2], a2_col).then_inc(weights_loaded, 16)
                for dst, src in ((bcol[:, :], b_col), (brow[:, :], b_row), (ba[:, :], ba_11)):
                    sp.dma_start(dst, src).then_inc(biases_loaded, 16)

                def load(g, c):
                    sp.dma_start(a_sb[:, :, c * CW:(c + 1) * CW],
                                 adj[g * GW:(g + 1) * GW, c * CW:(c + 1) * CW]
                                 .rearrange("(q p) n -> p q n", p=P)).then_inc(a_loaded[c], 16)

                for i in range(1, X_FIRST):
                    load_x(i)
                load(0, 0)
                for i in range(X_FIRST, G):
                    load_x(i)
                for c in range(1, CHUNKS):
                    load(0, c)
                sp.dma_start(diag[:, :], diagonal, allow_slow_non_contiguous=True).then_inc(diag_loaded, 16)

                def store(g):
                    sp.wait_ge(fin_step, FIN * (g + 1))
                    sp.dma_start(out_t[:, g * Q:(g + 1) * Q, :], out_sb[:, :, :]).then_inc(stored, 16)

                for g in range(1, G):
                    for c in range(CHUNKS):
                        sp.wait_ge(at_ready, PAIRS * (g - 1) + PPC * (c + 1))
                        sp.wait_ge(a_checked, PARTS * (CHUNKS * (g - 1) + c + 1))
                        load(g, c)
                    if g >= 2:
                        store(g - 2)
                for g in (G - 2, G - 1):
                    store(g)
                sp.wait_ge(stored, 16 * G)

            @block.gpsimd
            def _(pool):
                nc.gpsimd.memset(ident[:, :], 0.0).then_inc(consts_ready, 1)
                nc.gpsimd.memset(last_row[:, :], 0.0).then_inc(consts_ready, 1)
                nc.gpsimd.memset(e_last[:, :], 0.0).then_inc(consts_ready, 1)
                nc.gpsimd.memset(ones[:, :], 1.0).then_inc(consts_ready, 1)
                nc.gpsimd.memset(minus1[:, :], -1.0).then_inc(consts_ready, 1)
                nc.gpsimd.memset(minus_half[:, :], -0.5).then_inc(consts_ready, 1)
                nc.gpsimd.memset(half[:, :], 0.5).then_inc(consts_ready, 1)
                pool.wait_ge(consts_ready, 7)
                nc.gpsimd.affine_select(out=ident[:, :], in_=ident[:, :], compare_op=ALU.not_equal, fill=1.0,
                                        base=0, pattern=[[-1, P]], channel_multiplier=1).then_inc(consts_ready, 1)
                nc.gpsimd.affine_select(out=last_row[:, :], in_=last_row[:, :], compare_op=ALU.not_equal, fill=-1.0,
                                        base=1 - P, pattern=[[0, P]], channel_multiplier=1).then_inc(consts_ready, 1)
                nc.gpsimd.memset(e_last[0:1, P - 1:P], 1.0).then_inc(consts_ready, 1)
                pool.wait_ge(vec_const, CS_READY)
                nc.gpsimd.tensor_tensor(norm_u[:, :], cs[:, 1:2], half[:, :], ALU.pow).then_inc(norm_ready, 1)

                def root(i):
                    pool.wait_ge(norm0, 2 * i + 2)
                    if i >= 2:
                        pool.wait_ge(xhat_ready, i - 1)
                    nc.gpsimd.tensor_tensor(rstd[:, i % 2, :], rv[:, i % 2, :],
                                            minus_half[:, :].broadcast_to([P, Q]), ALU.pow).then_inc(rstd_ready, 1)

                def features(i):
                    ts = slice(Q * i, Q * (i + 1))
                    pool.wait_ge(exps_ready, 2 * i + 1)
                    pool.wait_ge(xhat_ready, i + 1)
                    nc.gpsimd.tensor_tensor(feat[:, ts, 0:D - 1], xhat[:, ts, 0:D - 1],
                                            v_exp[:, ts].unsqueeze(2).broadcast_to([P, Q, D - 1]),
                                            ALU.mult).then_inc(feat_ready, 1)
                    nc.gpsimd.tensor_copy(feat[:, ts, D - 1], v_exp[:, ts]).then_inc(feat_ready, 1)

                def split_features(i):
                    pool.wait_ge(feat_ready, 2 * i + 2)
                    ts, hs = slice(Q * i + 2, Q * i + 4), slice(2 * i, 2 * i + 2)
                    nc.gpsimd.tensor_copy(fh[:, hs, :], feat[:, ts, :]).then_inc(parts_ready, 1)
                    pool.wait_ge(parts_ready, 2 * i + 1)
                    nc.gpsimd.tensor_tensor(fl[:, hs, :], feat[:, ts, :], fh[:, hs, :],
                                            ALU.subtract).then_inc(parts_ready, 1)

                def low(g, p):
                    k = SPLIT.index(p)
                    pool.wait_ge(ph_ready, N_SPLIT * (g - 1) + k + 1)
                    nc.gpsimd.tensor_tensor(pl[:, k % NH, :], e_sb[:, p % NE, :], ph[:, k % NH, :],
                                            ALU.subtract).then_inc(pl_ready, 1)

                def root_of_group(g):
                    pool.wait_ge(fin_step, FIN * g + FIN - 1)
                    nc.gpsimd.tensor_tensor(frstd[:, :], frv[:, :],
                                            minus_half[:, :].broadcast_to([P, Q]), ALU.pow).then_inc(rstd_ready, 1)

                for slot in range(FIRST_SLOT, PAIRS):
                    if (i := quad_at(slot, VARY)) is not None:
                        root(i)
                    if (i := quad_at(slot, FEATURES)) is not None:
                        features(i)
                    if (i := quad_at(slot, SPLIT_FEATURES)) is not None:
                        split_features(i)
                with pool.Fori(1, G) as g:
                    for p in SPLIT:
                        low(g, p)
                        if p == ROOT_AT:
                            root_of_group(g - 1)
                root_of_group(G - 1)

            @block.scalar
            def _(act):
                act.dma_start(w_nat[:, :], W).then_inc(weights_loaded, 16)
                act.dma_start(wv[:, :], Wv).then_inc(weights_loaded, 16)

                def copy_xt(i):
                    act.wait_ge(xt_ready, i + 1)
                    if i >= 2:
                        act.wait_ge(y0_ready, i - 1)
                    nc.scalar.copy(x_tr[:, i % 2, :], ps_xt[:, :]).then_inc(xt_copied, 1)

                def square(i):
                    act.wait_ge(y0_kept, i + 1)
                    if i >= 2:
                        act.wait_ge(norm0, 2 * (i - 2) + 1)
                    nc.scalar.activation(sq[:, i % 2, :].rearrange("p (q d) -> p q d", q=Q),
                                         xhat[:, Q * i:Q * (i + 1), :],
                                         ACT.Square).then_inc(sq_ready, 1)

                def column_exps(i):
                    act.wait_ge(xhat_ready, i + 1)
                    if i == 0:
                        act.wait_ge(vec_const, BIASES)
                    ts = slice(Q * i, Q * (i + 1))
                    nc.scalar.activation(v_exp[:, ts], st_cols[:, ts, 1], ACT.Exp, bias=bias[:, 1:2],
                                         scale=SLOPE).then_inc(exps_ready, 1)
                    nc.scalar.activation(w_exp[:, ts], st_cols[:, ts, 1], ACT.Exp, bias=bias[:, 0:1],
                                         scale=1 - SLOPE).then_inc(exps_ready, 1)

                def row_exps(g, odd, src=ps_row):
                    act.wait_ge(row_ready, g + 1)
                    nc.scalar.activation(R[:, int(odd), :], src[:, :], ACT.Exp, bias=bias[:, 3:4],
                                         scale=1 - SLOPE).then_inc(r_ready, 1)

                def copy_acc(odd):
                    nc.scalar.copy(acc_t[:, :], ps_acc[odd][:, :]).then_inc(acc_copied, 1)

                def check_values(g, n, first):
                    c, part = divmod(n, PARTS)
                    if part == 0:
                        act.wait_ge(a_loaded[c], 16 * (g + 1))
                    if not (first and n == 0):
                        act.wait_ge(a_checked, CHUNKS * PARTS * g + n)
                    qs = slice(part * Q // PARTS, (part + 1) * Q // PARTS)
                    nc.scalar.activation(a_junk[:, :, :], a_sb[:, qs, c * CW:(c + 1) * CW], ACT.Square,
                                         bias=minus_half[:, :],
                                         accum_out=a_sum[:, bass.ds(g * CHUNKS * PARTS + n, 1)]).then_inc(a_checked, 1)

                def pair(g, p, odd, first=False, last=False):
                    if p == 0:
                        act.wait_ge(r_ready, g + 1)
                    if first and p % 2 == 0:
                        act.wait_ge(exps_ready, p + 2)
                    if p not in (BY_VECTOR0 if first else BY_VECTOR):
                        if not (first and p < NE):
                            act.wait_ge(mm_done, PAIRS * g + p - NE + 1)
                        for side in range(2):
                            ins = nc.scalar.activation(e_sb[:, p % NE, side * GW:(side + 1) * GW],
                                                       R[:, int(odd), :], ACT.Relu, bias=minus1[:, :],
                                                       scale=w_exp[:, 2 * p + side:2 * p + side + 1])
                        ins.then_inc(e_ready, 1)
                    if p == COPY_AT and not first:
                        act.wait_ge(mm_done, PAIRS * g)
                        copy_acc(not odd)
                    if p == R_AT and not first and not last:
                        act.wait_ge(e_ready, by_scalar(g, -1, False))
                        act.wait_ge(ev_ready, by_vector(g, -1, False))
                        row_exps(g + 1, not odd)
                    if p % (PPC // PARTS) == CHECK_AT:
                        check_values(g, p // (PPC // PARTS), first)

                for slot in range(FIRST_SLOT, PAIRS):
                    if (i := quad_at(slot, COPY)) is not None:
                        copy_xt(i)
                    if (i := quad_at(slot, SQUARE)) is not None:
                        square(i)
                    if (i := quad_at(slot, EXPS)) is not None:
                        column_exps(i)
                    if slot == EXPS:
                        row_exps(0, False, ps_acc[0])
                    if slot >= 0:
                        pair(0, slot, odd=False, first=True)
                    if slot == R1_AT:
                        row_exps(1, True, ps_acc[1])
                for p in range(PAIRS):
                    pair(1, p, odd=True)
                with act.Fori(1, G // 2 - 1) as k:
                    for odd in (False, True):
                        for p in range(PAIRS):
                            pair(2 * k + odd, p, odd)
                for g in (G - 2, G - 1):
                    for p in range(PAIRS):
                        pair(g, p, odd=g % 2 == 1, last=g == G - 1)
                act.wait_ge(mm_done, PAIRS * G)
                copy_acc(odd=True)

            @block.vector
            def _(dve):
                done = [0]

                def step(ins, s=vec_const):
                    done[0] += 1
                    ins.then_inc(s, 1)
                    dve.wait_ge(s, done[0])

                def centre(dst, src, c):
                    step(nc.vector.reduce_sum(mean[:, c:c + 1], src, AX))
                    step(nc.vector.tensor_scalar(mean[:, c + 1:c + 2], mean[:, c:c + 1], 1.0 / D, None, ALU.mult))
                    step(nc.vector.tensor_scalar(dst, src, mean[:, c + 1:c + 2], None, ALU.subtract))

                dve.wait_ge(consts_ready, 10)
                step(nc.vector.tensor_tensor(less_last[:, :], ident[:, :], last_row[:, :], ALU.add))
                dve.wait_ge(weights_loaded, 16 * 4)
                step(nc.vector.tensor_tensor(m0[:, :], wv[:, :], ident[:, :], ALU.add))
                centre(m0c, m0[:, :], 0)
                assert done[0] == M0_READY
                dve.wait_ge(pe_const, 1)
                step(nc.vector.tensor_copy(u[:, :], ps_misc[:, D:D + 2]))
                nc.vector.tensor_tensor(bb[:, 0:1], acol[:, 0:1], acol[:, 1:2], ALU.add).then_inc(vec_const, 1)
                done[0] += 1
                step(nc.vector.tensor_tensor(bb[:, 1:2], u[:, 1:2], u[:, 1:2], ALU.mult))
                dve.wait_ge(biases_loaded, 16 * 3)
                step(nc.vector.tensor_tensor(bb[:, 0:1], bb[:, 0:1], bcol[:, :], ALU.mult))
                assert done[0] == U_READY
                step(nc.vector.tensor_copy(w_t[:, :], ps_misc[:, 0:D]))
                dve.wait_ge(pe_const, 2)
                step(nc.vector.tensor_copy(m0c_t[:, :], ps_misc[:, 2 * D:3 * D]))
                assert done[0] == M0T_READY
                dve.wait_ge(pe_const, 3)
                step(nc.vector.tensor_copy(um, ps_misc[:, D:D + 2]))
                step(nc.vector.tensor_copy(cs[:, :], ps_misc[:, D + 2:D + 4]))
                assert done[0] == CS_READY

                def biases():
                    dve.wait_ge(norm_ready, 1)
                    nc.vector.tensor_scalar(bias[:, 0:1], norm_u[:, :], (SLOPE - 1) * D ** 0.5, None,
                                            ALU.mult).then_inc(vec_const, 1)
                    nc.vector.tensor_scalar(bias[:, 1:2], norm_u[:, :], -SLOPE * D ** 0.5, float(np.log(V_SCALE)),
                                            ALU.mult, ALU.add).then_inc(vec_const, 1)
                    done[0] += 2
                    step(nc.vector.scalar_tensor_tensor(out=bias[:, 2:3], in0=norm_u[:, :], scalar=D ** 0.5,
                                                        in1=cs[:, 0:1], op0=ALU.mult, op1=ALU.add))
                    nc.vector.tensor_scalar(bias[:, 3:4], bias[:, 2:3], 1 - SLOPE, None,
                                            ALU.mult).then_inc(vec_const, 1)
                    done[0] += 1
                    step(nc.vector.tensor_scalar(bias[:, 4:5], bias[:, 2:3], -1.0, MAX_S, ALU.mult, ALU.add))
                    assert done[0] == BIASES
                    nc.vector.tensor_copy(ident16[:, :], ident[:, :]).then_inc(vec_const, 1)
                    done[0] += 1

                def weights2():
                    dve.wait_ge(pe_const, 4)
                    step(nc.vector.tensor_copy(w2[:, :], ps_w2[:, 0:D]))
                    assert done[0] == W2_READ
                    centre(w2c, w2[:, :], 2)
                    step(nc.vector.tensor_copy(pick_den, ident[:, P - 1:P]))

                def keep(i):
                    dve.wait_ge(y0_ready, i + 1)
                    nc.vector.tensor_copy(xhat_st[:, Q * i:Q * (i + 1), :], ps_quad[:, :, 0:D + 2]).then_inc(y0_kept, 1)

                def variance(i):
                    k = i % 2
                    dve.wait_ge(sq_ready, i + 1)
                    if i >= 2:
                        dve.wait_ge(rstd_ready, i - 1)
                    nc.vector.reduce_sum(ss[:, k, :], sq[:, k, :].rearrange("p (q d) -> p q d", q=Q),
                                         AX).then_inc(norm0, 1)
                    dve.wait_ge(norm0, 2 * i + 1)
                    nc.vector.tensor_scalar(rv[:, k, :], ss[:, k, :], 1.0 / D, EPS, ALU.mult,
                                            ALU.add).then_inc(norm0, 1)

                def divide(i):
                    k = i % 2
                    ts = slice(Q * i, Q * (i + 1))
                    dve.wait_ge(rstd_ready, i + 1)
                    nc.vector.tensor_tensor(xhat_st[:, ts, :], xhat_st[:, ts, :],
                                            rstd[:, k, :].unsqueeze(2).broadcast_to([P, Q, D + 2]),
                                            ALU.mult).then_inc(xhat_ready, 1)

                def diagonals(g, first=False):
                    if first:
                        dve.wait_ge(xhat_ready, 1)
                    else:
                        dve.wait_ge(row_ready, g)
                    nc.vector.scalar_tensor_tensor(out=s_diag[:, :, :],
                                                   in0=st_cols[:, bass.ds(g * Q, Q), 0:1].broadcast_to([P, Q, P]),
                                                   scalar=bias[:, 4:5],
                                                   in1=ident[:, :].unsqueeze(1).broadcast_to([P, Q, P]),
                                                   op0=ALU.min, op1=ALU.mult).then_inc(diag_ready, 1)

                def finish(g, n, first=False):
                    if n == 0:
                        dve.wait_ge(fin_mm, g + 1)
                    else:
                        dve.wait_ge(fin_step, FIN * g + n)
                    if n == 0:
                        ins = nc.vector.tensor_scalar(den[:, :], ps_quad[:, :, D], FLT_MIN, None, ALU.max)
                    elif n == 1:
                        ins = nc.vector.reciprocal(rden[:, :], den[:, :])
                    elif n == 2:
                        ins = nc.vector.tensor_tensor(y[:, :, :], ps_quad[:, :, 0:D],
                                                      rden[:, :].unsqueeze(2).broadcast_to([P, Q, D]), ALU.mult)
                    elif n == 3:
                        ins = nc.vector.tensor_tensor(y[:, :, :], y[:, :, :], xhat[:, bass.ds(g * Q, Q), :], ALU.add)
                    elif n == 4:
                        ins = nc.vector.tensor_tensor(ysq[:, :, :], y[:, :, :], y[:, :, :], ALU.mult)
                    elif n == 5:
                        ins = nc.vector.reduce_sum(fss[:, :], ysq[:, :, :], AX)
                    elif n == 6:
                        ins = nc.vector.tensor_scalar(frv[:, :], fss[:, :], 1.0 / D, EPS, ALU.mult, ALU.add)
                    else:
                        dve.wait_ge(rstd_ready, G + g + 1)
                        if not first:
                            dve.wait_ge(stored, 16 * g)
                        ins = nc.vector.tensor_tensor(out_sb[:, :, :], y[:, :, :],
                                                      frstd[:, :].unsqueeze(2).broadcast_to([P, Q, D]), ALU.mult)
                    ins.then_inc(fin_step, 1)

                def high(g, p):
                    dve.wait_ge(p_ready, PAIRS * g + p + 1)
                    nc.vector.tensor_copy(ph[:, SPLIT.index(p) % NH, :], e_sb[:, p % NE, :]).then_inc(ph_ready, 1)

                def pair(g, p, odd, first=False):
                    e = e_sb[:, p % NE, :]
                    own = p in (BY_VECTOR0 if first else BY_VECTOR)
                    if own:
                        dve.wait_ge(r_ready, g + 1)
                        if first:
                            dve.wait_ge(exps_ready, 2 * (p // 2) + 2)
                        if not (first and p < NE):
                            dve.wait_ge(mm_done, PAIRS * g + p - NE + 1)
                        for side in range(2):
                            ins = nc.vector.tensor_scalar(e[:, side * GW:(side + 1) * GW], R[:, int(odd), :],
                                                          w_exp[:, 2 * p + side:2 * p + side + 1], 1.0, ALU.mult,
                                                          ALU.max)
                        ins.then_inc(ev_ready, 1)
                        plus = 0.0
                    else:
                        plus = 1.0
                    if p - 1 in SPLIT and not first:
                        high(g, p - 1)
                    if own:
                        dve.wait_ge(ev_ready, by_vector(g, p, first))
                    else:
                        dve.wait_ge(e_ready, by_scalar(g, p, first))
                    dve.wait_ge(at_ready, PAIRS * g + p + 1)
                    nc.vector.scalar_tensor_tensor(out=e, in0=e, scalar=plus, in1=ps_at_int[p % NA],
                                                   op0=ALU.add, op1=ALU.mult).then_inc(p_ready, 1)

                def group(g, odd, second=False, last=False):
                    for p in range(PAIRS):
                        pair(g, p, odd)
                        if FIN_AT <= p < FIN_AT + FIN - 1:
                            finish(g - 1, p - FIN_AT, first=second)
                        if p == PAIRS - 1:
                            finish(g - 1, FIN - 1, first=second)
                        if p == DIAG_AT and not last:
                            diagonals(g + 1)
                    high(g, PAIRS - 1)

                for slot in range(FIRST_SLOT, PAIRS):
                    if (i := quad_at(slot, KEEP)) is not None:
                        keep(i)
                    if slot == KEEP:
                        weights2()
                    if (i := quad_at(slot, VARY)) is not None:
                        variance(i)
                    if slot == VARY:
                        biases()
                    if (i := quad_at(slot, DIVIDE)) is not None:
                        divide(i)
                    if slot == DIVIDE:
                        diagonals(0, first=True)
                    if slot >= 0:
                        pair(0, slot, odd=False, first=True)
                    if slot == DIAG1_AT:
                        diagonals(1)
                group(1, odd=True, second=True)
                with dve.Fori(1, G // 2 - 1) as k:
                    for odd in (False, True):
                        group(2 * k + odd, odd)
                group(G - 2, odd=False)
                group(G - 1, odd=True, last=True)

                done[0] = 0
                dve.wait_ge(a_checked, G * CHUNKS * PARTS)
                dve.wait_ge(diag_loaded, 16)
                nc.vector.tensor_reduce(ext[:, 0:1], st_cols[:, :, 1], AX, ALU.min).then_inc(verdict, 1)
                nc.vector.tensor_reduce(ext[:, 1:2], st_cols[:, :, 0], AX, ALU.max).then_inc(verdict, 1)
                nc.vector.tensor_reduce(ext[:, 2:3], st_cols[:, :, 0], AX, ALU.min).then_inc(verdict, 1)
                nc.vector.reduce_max(checks[:, 0:1], a_sum[:, :], AX).then_inc(verdict, 1)
                nc.vector.tensor_reduce(checks[:, 1:2], diag[:, :], AX, ALU.min).then_inc(verdict, 1)
                done[0] += 5
                dve.wait_ge(verdict, done[0])
                nc.vector.scalar_tensor_tensor(out=checks[:, 2:3], in0=norm_u[:, :], scalar=D ** 0.5, in1=ext[:, 0:1],
                                               op0=ALU.mult, op1=ALU.subtract).then_inc(verdict, 1)
                nc.vector.tensor_tensor(checks[:, 3:4], ext[:, 1:2], bias[:, 2:3], ALU.add).then_inc(verdict, 1)
                nc.vector.scalar_tensor_tensor(out=checks[:, 4:5], in0=ext[:, 2:3], scalar=-1.0, in1=bias[:, 2:3],
                                               op0=ALU.mult, op1=ALU.subtract).then_inc(verdict, 1)
                done[0] += 3
                dve.wait_ge(verdict, done[0])
                nc.vector.tensor_scalar(checks[:, 0:1], checks[:, 0:1], Q // PARTS * CW / 4.0, None,
                                        ALU.is_le).then_inc(verdict, 1)
                nc.vector.tensor_scalar(checks[:, 1:2], checks[:, 1:2], 1.0, None, ALU.is_ge).then_inc(verdict, 1)
                for c, most in ((2, MAX_BELOW), (3, MAX_S), (4, -MIN_S)):
                    nc.vector.tensor_scalar(checks[:, c:c + 1], checks[:, c:c + 1], most, None,
                                            ALU.is_le).then_inc(verdict, 1)
                done[0] += 5
                dve.wait_ge(verdict, done[0])
                step(nc.vector.reduce_sum(held[:, :], checks[:, :], AX), verdict)
                assert done[0] == CHECKS_READY
                for n in range(FIN):
                    finish(G - 1, n)
                dve.wait_ge(verdict_pe, 1)
                total = float(5 * P)
                if force_general:
                    total += 1.0
                step(nc.vector.tensor_scalar(flag[:, :], ps_acc[0][0:1, 0:1], total, None, ALU.not_equal), verdict)

            @block.tensor
            def _(pe):
                pe.wait_ge(consts_ready, 10)

                def x_transposed(i):
                    pe.wait_ge(x_loaded[i], 16)
                    if i >= 1:
                        pe.wait_ge(xt_copied, i)
                    for q in range(Q):
                        ins = nc.tensor.transpose(ps_xt[:, q * P:(q + 1) * P], x_sb[:, Q * i + q, :], ident[:, :])
                    ins.then_inc(xt_ready, 1)

                def layer0(i):
                    pe.wait_ge(xt_copied, i + 1)
                    if i == 0:
                        pe.wait_ge(vec_const, CS_READY)
                    else:
                        pe.wait_ge(y0_kept, i)
                    for q in range(Q):
                        ins = nc.tensor.matmul(ps_quad[:, q, 0:D + 2],
                                               x_tr[:, i % 2, q * P:(q + 1) * P], m0c_um[:, :], start=True, stop=True)
                    ins.then_inc(y0_ready, 1)

                def spread(g, dst=ps_row, first=False, second=False, third=False):
                    pe.wait_ge(diag_ready, g + 1)
                    if first:
                        pe.wait_ge(vec_const, W2_READ)
                    elif second:
                        pe.wait_ge(xt_copied, G)
                    elif third:
                        pe.wait_ge(y0_kept, G)
                    else:
                        pe.wait_ge(fin_step, FIN * (g - 3) + 3)
                    nc.tensor.matmul(dst[:, :], ones[:, :], s_diag[:, :, :].rearrange("p q n -> p (q n)"),
                                     start=True, stop=True).then_inc(row_ready, 1)

                def weights():
                    pe.wait_ge(weights_loaded, 16 * 4)
                    nc.tensor.transpose(ps_misc[:, 0:D], w_nat[:, :], ident[:, :])
                    nc.tensor.matmul(ps_misc[:, D:D + 2], w_nat[:, :], acol[:, :], start=True,
                                     stop=True).then_inc(pe_const, 1)
                    pe.wait_ge(vec_const, U_READY + 1)
                    nc.tensor.transpose(ps_misc[:, 2 * D:3 * D], m0c, ident[:, :]).then_inc(pe_const, 1)
                    pe.wait_ge(vec_const, M0T_READY)
                    nc.tensor.matmul(ps_misc[:, D:D + 2], m0c_t[:, :], u[:, :], start=True, stop=True)
                    nc.tensor.matmul(ps_misc[:, D + 2:D + 4], ones[:, :], bb[:, :], start=True, stop=False,
                                     skip_group_check=True)
                    nc.tensor.matmul(ps_misc[:, D + 2:D + 3], ones[0:1, :], ba[:, :], start=False, stop=True,
                                     skip_group_check=True).then_inc(pe_const, 1)
                    nc.tensor.matmul(ps_w2[:, 0:D], less_last[:, :], w_t[:, :], start=True, stop=False)
                    nc.tensor.matmul(ps_w2[:, 0:D], e_last[:, :], brow[:, :], start=False,
                                     stop=True).then_inc(pe_const, 1)

                half_words = a_sb[:, :, :].rearrange("p q n -> p (q n)").bitcast(F16).rearrange(
                    "p (q n two) -> p q n two", q=Q, two=2)[:, :, :, 0]

                def pair(g, p, first=False):
                    if p % PPC == 0:
                        pe.wait_ge(a_loaded[p // PPC], 16 * (g + 1))
                    if first and p == 0:
                        pe.wait_ge(vec_const, BIASES + 1)
                    if not (first and p < NA):
                        pe.wait_ge(p_ready, PAIRS * g + p - NA + 1)
                    for side in range(2):
                        for q in range(Q):
                            j = (2 * p + side) * P
                            c = side * GW + q * P
                            ins = nc.tensor.transpose(ps_at[p % NA][:, c:c + P], half_words[:, q, j:j + P],
                                                      ident16[:, :])
                    ins.then_inc(at_ready, 1)

                def sums(g, p, odd, first=False, second=False, last=False):
                    if p == 0:
                        if first:
                            pe.wait_ge(r_ready, 1)
                        elif second:
                            pe.wait_ge(r_ready, 2)
                        else:
                            pe.wait_ge(acc_copied, g - 1)
                    split = p in SPLIT and not first
                    if first and p % 2 == 0:
                        pe.wait_ge(feat_ready, 2 * (p // 2 + 1))
                    if split:
                        k = SPLIT.index(p)
                        if second and k == 0:
                            pe.wait_ge(parts_ready, 2 * G)
                        pe.wait_ge(pl_ready, N_SPLIT * (g - 1) + k + 1)
                        passes = ((fl, ph), (fh, ph), (fh, pl))
                    elif last and p + AHEAD >= PAIRS:
                        pe.wait_ge(p_ready, PAIRS * g + p + 1)
                    for side in range(2):
                        j = 2 * p + side
                        cols = slice(side * GW, (side + 1) * GW)
                        if split:
                            for n, (f, w) in enumerate(passes):
                                ins = nc.tensor.matmul(ps_acc[odd][:, :], f[:, 2 * k + side, :], w[:, k % NH, cols],
                                                       start=False, stop=(j == T - 1 and n == 2))
                        else:
                            ins = nc.tensor.matmul(ps_acc[odd][:, :], feat[:, j, :], e_sb[:, p % NE, cols],
                                                   start=(j == 0), stop=(j == T - 1))
                    ins.then_inc(mm_done, 1)

                def project(g, last=False):
                    pe.wait_ge(acc_copied, g + 1)
                    if last:
                        pe.wait_ge(fin_step, FIN * (g - 1) + 3)
                    else:
                        pe.wait_ge(r_ready, g + 3)
                    for q in range(Q):
                        ins = nc.tensor.matmul(ps_quad[:, q, 0:D + 1], acc_t[:, q * P:(q + 1) * P], w2c_den[:, :],
                                               start=True, stop=True)
                    ins.then_inc(fin_mm, 1)

                def group(g, odd, second=False, last=False):
                    for p in range(PAIRS):
                        n = p + AHEAD
                        if n < PAIRS:
                            pair(g, n)
                        elif not last:
                            pair(g + 1, n - PAIRS)
                        sums(g, p, odd, second=second, last=last)
                        if p == PROJECT_AT:
                            project(g - 1, last=last)
                        if p == SPREAD_AT and not last:
                            spread(g + 1, third=second)

                for slot in range(FIRST_SLOT, PAIRS):
                    if (i := quad_at(slot, TURN)) is not None:
                        x_transposed(i)
                    if slot == FIRST_SLOT:
                        weights()
                    if (i := quad_at(slot, MULTIPLY)) is not None:
                        layer0(i)
                    if slot == SPREAD0_AT:
                        spread(0, dst=ps_acc[0], first=True)
                    n = slot + AHEAD
                    if n >= PAIRS:
                        pair(1, n - PAIRS)
                    elif n >= 0:
                        pair(0, n, first=True)
                    if slot >= 0:
                        sums(0, slot, odd=False, first=True)
                    if slot == SPREAD1_AT:
                        spread(1, dst=ps_acc[1], second=True)
                group(1, odd=True, second=True)
                group(2, odd=False)
                with pe.Fori(1, G // 2 - 1) as k:
                    for odd in (True, False):
                        group(2 * k + 2 - odd, odd)
                group(G - 1, odd=True, last=True)
                project(G - 1, last=True)
                pe.wait_ge(verdict, CHECKS_READY)
                nc.tensor.matmul(ps_acc[0][0:1, 0:1], held[:, :], ones[:, 0:1], start=True,
                                 stop=True).then_inc(verdict_pe, 1)

        xhat_t = p_parts[:, :, :, :].rearrange("p a b c -> p (a b c)").bitcast(F32)
        wq = sb("wq", [P, D])
        wk = sb("wk", [P, D])
        q_cur = sb("q_cur", [P, P])
        u2_rep = sb("u2_rep", [P, P])
        s_cur = sb("s_cur", [P, 1])
        s_col = sb("s_col", [P, T])
        neg_max = sb("neg_max", [P, 1])
        row_sum = sb("row_sum", [P, 1])
        a_row = a_sb[:, 0, :]
        scores_row = a_sb[:, 1, :].bitcast(F32)
        k_t = a_sb[:, 2, :].bitcast(F32)
        q_t = a_sb[:, 3, :].bitcast(F32)
        pairs_flat = e_sb[:, :, :].rearrange("p n c -> p (n c)")
        p_t = pairs_flat[:, 0:N]
        mask = pairs_flat[:, N:2 * N]
        values = feat
        yg, yg2 = y[:, 0, :], y[:, 1, :]

        g_loaded = sem("g_loaded")
        g_made = sem("g_made")
        g_kept = sem("g_kept")
        g_small = sem("g_small")
        g_adj = [sem(f"g_adj{n}") for n in range(2)]
        g_query = [sem(f"g_query{n}") for n in range(2)]
        g_prod = [sem(f"g_prod{n}") for n in range(2)]
        g_vec = [sem(f"g_vec{n}") for n in range(2)]
        g_exp = [sem(f"g_exp{n}") for n in range(2)]
        g_pt = [sem(f"g_pt{n}") for n in range(2)]
        g_pt_kept = [sem(f"g_pt_kept{n}") for n in range(2)]
        g_sums = [sem(f"g_sums{n}") for n in range(2)]
        g_rstd = [sem(f"g_rstd{n}") for n in range(2)]
        g_stored = sem("g_stored")
        KEPT = [4 * G, 7 * G]
        SCORED = [16, 10]
        VARIED = [25, 19]
        ROWS = [26, 20]

        def if_general(eng):
            return eng.If(eng.value_load(flag[0:1, 0:1]) != 0)

        with nc.Block() as block:

            @block.tensor
            def _(pe):
                with if_general(pe):
                    made = [0]

                    def product(ins):
                        made[0] += 1
                        ins.then_inc(g_made, 1)
                        pe.wait_ge(g_kept, made[0])

                    def turned(src):
                        for i in range(G):
                            for q in range(Q):
                                ins = nc.tensor.transpose(bank[0][:, q * P:(q + 1) * P], src[:, Q * i + q, :],
                                                          ident[:, :])
                            product(ins)

                    def by_rows(w):
                        for i in range(G):
                            product(nc.tensor.matmul(bank[0][:, :], w[:, :], xhat_t[:, i * GW:(i + 1) * GW],
                                                     start=True, stop=True))

                    def by_cols(w, bias_row):
                        for i in range(G):
                            for q in range(Q):
                                t = Q * i + q
                                dst = bank[0][:, q * P:(q + 1) * P]
                                ins = nc.tensor.matmul(dst, xhat_t[:, t * P:(t + 1) * P], w[:, :], start=True,
                                                       stop=bias_row is None)
                                if bias_row is not None:
                                    ins = nc.tensor.matmul(dst, ones[0:1, :], bias_row[:, :], start=False, stop=True)
                            product(ins)

                    def tiles(n):
                        with pe.Fori(0, T) as t:
                            if n == 0:
                                pe.wait_ge(g_query[n], t + 1)
                                for c in range(G):
                                    nc.tensor.matmul(bank[c][:, :], q_cur[:, :], k_t[:, c * GW:(c + 1) * GW],
                                                     start=True, stop=True).then_inc(g_prod[n], 1)
                            pe.wait_ge(g_exp[n], t + 1)
                            for c in range(G):
                                for q in range(Q):
                                    j = Q * c + q
                                    ins = nc.tensor.transpose(bank[c][:, q * P:(q + 1) * P],
                                                              scores_row[:, j * P:(j + 1) * P], ident[:, :])
                                ins.then_inc(g_pt[n], 1)
                            pe.wait_ge(g_pt_kept[n], G * (t + 1))
                            for j in range(T):
                                ins = nc.tensor.matmul(bank[0][:, 0:D], p_t[:, j * P:(j + 1) * P], values[:, j, :],
                                                       start=(j == 0), stop=(j == T - 1))
                            ins.then_inc(g_sums[n], 1)
                            pe.wait_ge(g_vec[n], ROWS[n] * (t + 1))

                    pe.wait_ge(g_loaded, 32)
                    turned(x_sb)
                    by_rows(wq)
                    by_rows(wk)
                    by_cols(wv, None)
                    tiles(0)
                    turned(xhat)
                    pe.wait_ge(g_small, 1)
                    by_rows(u2_rep)
                    by_cols(w_t, brow)
                    assert made[0] == KEPT[1]
                    for t in range(T):
                        ins = nc.tensor.matmul(bank[1][:, t:t + 1], xhat_t[:, t * P:(t + 1) * P], u[:, 0:1],
                                               start=True, stop=True)
                    ins.then_inc(g_made, 1)
                    tiles(1)

            @block.scalar
            def _(act):
                with if_general(act):
                    kept = [0]

                    def keep(dst):
                        kept[0] += 1
                        act.wait_ge(g_made, kept[0])
                        nc.scalar.copy(dst, bank[0][:, :]).then_inc(g_kept, 1)

                    def keep_all(dst):
                        for i in range(G):
                            keep(dst(i))

                    def cols(buf):
                        return lambda i: buf[:, i * GW:(i + 1) * GW]

                    def by_tile(buf):
                        return lambda i: buf[:, Q * i:Q * (i + 1), :].rearrange("p q d -> p (q d)")

                    def tiles(n):
                        with act.Fori(0, T) as t:
                            act.dma_start(a_row, adj[bass.ds(t * P, P), :]).then_inc(g_adj[n], 16)
                            act.wait_ge(g_vec[n], ROWS[n] * t + SCORED[n])
                            nc.scalar.activation(scores_row, scores_row, ACT.Exp,
                                                 accum_out=row_sum[:, :]).then_inc(g_exp[n], 1)
                            for c in range(G):
                                act.wait_ge(g_pt[n], G * t + c + 1)
                                nc.scalar.copy(p_t[:, c * GW:(c + 1) * GW], bank[c][:, :]).then_inc(g_pt_kept[n], 1)
                            act.wait_ge(g_vec[n], ROWS[n] * (t + 1))
                            if n == 1:
                                act.dma_start(out_t[:, bass.ds(t, 1), :], out_sb[:, 0:1, :]).then_inc(g_stored, 16)
                                act.wait_ge(g_stored, 16 * (t + 1))

                    keep_all(cols(xhat_t))
                    keep_all(cols(q_t))
                    keep_all(cols(k_t))
                    keep_all(by_tile(values))
                    assert kept[0] == KEPT[0]
                    tiles(0)
                    keep_all(cols(xhat_t))
                    keep_all(cols(k_t))
                    keep_all(by_tile(values))
                    tiles(1)

            @block.sync
            def _(sp):
                with if_general(sp):
                    sp.dma_start(wq[:, :], Wq).then_inc(g_loaded, 16)
                    sp.dma_start(wk[:, :], Wk).then_inc(g_loaded, 16)
                    sp.wait_ge(g_loaded, 32)

            @block.gpsimd
            def _(pool):
                with if_general(pool):
                    for n in range(2):
                        with pool.Fori(0, T) as t:
                            pool.wait_ge(g_vec[n], ROWS[n] * t + VARIED[n])
                            nc.gpsimd.tensor_tensor(frstd[:, 0:1], frv[:, 0:1], minus_half[:, :],
                                                    ALU.pow).then_inc(g_rstd[n], 1)

            @block.vector
            def _(dve):
                with if_general(dve):
                    def tiles(n):
                        dve.wait_ge(g_kept, KEPT[n])
                        with dve.Fori(0, T) as t:
                            done = [0]

                            def step(ins):
                                done[0] += 1
                                ins.then_inc(g_vec[n], 1)
                                dve.wait_ge(g_vec[n], ROWS[n] * t + done[0])

                            if n == 0:
                                step(nc.vector.tensor_copy(q_cur[:, :], q_t[:, bass.ds(t * P, P)]))
                                dve.sem_inc(g_query[n], 1)
                                dve.wait_ge(g_adj[n], 16 * (t + 1))
                                step(nc.vector.tensor_copy(mask, a_row))
                                own = pairs_flat[:, bass.ds(t * P + N, P)]
                                step(nc.vector.tensor_tensor(own, own, ident[:, :], ALU.add))
                                step(nc.vector.tensor_scalar(mask, mask, -1.0, -1.0, ALU.add, ALU.max))
                                step(nc.vector.tensor_scalar(mask, mask, 1.0, FLT_MAX, ALU.min, ALU.mult))
                                for c in range(G):
                                    dve.wait_ge(g_prod[n], G * t + c + 1)
                                    cc = slice(c * GW, (c + 1) * GW)
                                    step(nc.vector.tensor_tensor(scores_row[:, cc], bank[c][:, :], mask[:, cc],
                                                                 ALU.add))
                            else:
                                step(nc.vector.tensor_copy(s_cur[:, :], s_col[:, bass.ds(t, 1)]))
                                step(nc.vector.tensor_scalar(scores_row, k_t, s_cur[:, :], None, ALU.add))
                                step(nc.vector.scalar_tensor_tensor(out=scores_row, in0=scores_row, scalar=SLOPE,
                                                                    in1=scores_row, op0=ALU.mult, op1=ALU.max))
                                dve.wait_ge(g_adj[n], 16 * (t + 1))
                                step(nc.vector.tensor_scalar(mask, a_row, 0.0, None, ALU.is_gt))
                                step(nc.vector.tensor_tensor(scores_row, scores_row, mask, ALU.mult))
                                step(nc.vector.tensor_scalar(mask, mask, -1.0, NEG, ALU.add, ALU.mult))
                                step(nc.vector.tensor_tensor(scores_row, scores_row, mask, ALU.add))
                            step(nc.vector.reduce_max(neg_max[:, :], scores_row, AX))
                            step(nc.vector.tensor_scalar(neg_max[:, :], neg_max[:, :], -1.0, None, ALU.mult))
                            step(nc.vector.tensor_scalar(scores_row, scores_row, neg_max[:, :], -FLT_MAX, ALU.add,
                                                         ALU.max))
                            assert done[0] == SCORED[n]
                            dve.wait_ge(g_sums[n], t + 1)
                            step(nc.vector.reciprocal(rden[:, 0:1], row_sum[:, :]))
                            step(nc.vector.tensor_scalar(yg, bank[0][:, 0:D], rden[:, 0:1], None, ALU.mult))
                            x_in = x_sb if n == 0 else xhat
                            step(nc.vector.tensor_tensor(y[:, 0:1, :], y[:, 0:1, :], x_in[:, bass.ds(t, 1), :],
                                                         ALU.add))
                            step(nc.vector.reduce_sum(mean[:, 0:1], yg, AX))
                            step(nc.vector.tensor_scalar(mean[:, 1:2], mean[:, 0:1], 1.0 / D, None, ALU.mult))
                            step(nc.vector.tensor_scalar(yg, yg, mean[:, 1:2], None, ALU.subtract))
                            step(nc.vector.tensor_tensor(yg2, yg, yg, ALU.mult))
                            step(nc.vector.reduce_sum(fss[:, 0:1], yg2, AX))
                            step(nc.vector.tensor_scalar(frv[:, 0:1], fss[:, 0:1], 1.0 / D, EPS, ALU.mult, ALU.add))
                            assert done[0] == VARIED[n]
                            dve.wait_ge(g_rstd[n], t + 1)
                            dst = xhat[:, bass.ds(t, 1), :] if n == 0 else out_sb[:, 0:1, :]
                            step(nc.vector.tensor_scalar(dst, y[:, 0:1, :], frstd[:, 0:1], None, ALU.mult))
                            assert done[0] == ROWS[n]

                    tiles(0)
                    nc.vector.tensor_scalar(u2_rep[:, :], ones[:, :], u[:, 1:2], None, ALU.mult).then_inc(g_small, 1)
                    dve.wait_ge(g_kept, KEPT[1])
                    dve.wait_ge(g_made, KEPT[1] + 1)
                    nc.vector.tensor_scalar(s_col[:, :], bank[1][:, 0:T], cs[:, 0:1], None,
                                            ALU.add).then_inc(g_small, 1)
                    dve.wait_ge(g_small, 2)
                    tiles(1)


_INS = ['x', 'adj', 'L0_gnn_Wq', 'L0_gnn_Wk', 'L0_gnn_Wv', 'L1_gnn_W', 'L1_gnn_b_W', 'L1_gnn_a_vec', 'L1_gnn_b_a']


def kernel(**inputs):
    import numpy as _np
    import concourse.bacc as _bacc
    from concourse import mybir as _mybir
    from concourse.bass_utils import run_bass_kernel_spmd as _run

    nc = _bacc.Bacc("TRN2", target_bir_lowering=False, num_devices=1)
    arrays, args = {}, []
    for name in _INS:
        a = _np.ascontiguousarray(inputs[name])
        arrays[f"in_{name}_dram"] = a
        args.append(nc.dram_tensor(f"in_{name}_dram", a.shape, _mybir.dt.from_np(a.dtype), kind="ExternalInput").ap())
    out = nc.dram_tensor("out_0_dram", inputs["x"].shape, _mybir.dt.float32, kind="ExternalOutput").ap()
    graph_layers(nc, args[0], args[1], args[2], args[3], args[4], args[5], args[6], args[7], args[8], out)
    r = _run(nc, [arrays], core_ids=[0])
    return r.results[0]["out_0_dram"]
```
